# Optimizing a Trainium2 kernel written in Bass

```python
import numpy as np
import jax
import jax.numpy as jnp

def _softmax(x, axis=-1):
    return jax.nn.softmax(x, axis=axis)

def _gelu(x):
    return jax.nn.gelu(x, approximate=True)

def _silu(x):
    return jax.nn.silu(x)

def _sigmoid(x):
    return jax.nn.sigmoid(x)

def _layernorm(x, axis=-1, eps=1e-05):
    m = jnp.mean(x, axis=axis, keepdims=True)
    v = jnp.var(x, axis=axis, keepdims=True)
    return (x - m) / jnp.sqrt(v + eps)

def _scatter_add(tgt, idx, src, axis=0):
    return tgt.at[idx].add(src)

def _segment_sum(src, seg, n):
    return jax.ops.segment_sum(src, seg, n)
kernel_name = 'mk_decoder_postln_d1_seqx_r8_21712d'

def setup_inputs(seed: int=0):
    np.random.seed(seed)
    _w = jnp.asarray

    def _rec_inputs():
        import jax
        import jax.numpy as jnp
        _rk = jax.random.key(seed)
        x = -0.000125 + 0.9999 * jax.random.normal(jax.random.fold_in(_rk, 1), (16, 128, 256), jnp.float32)
        _lenS = 128 - jax.random.randint(jax.random.fold_in(_rk, 7), (16,), 0, max(1, 128 // 4) + 1, jnp.int32)
        _lenS2 = 128 - jax.random.randint(jax.random.fold_in(_rk, 8), (16,), 0, max(1, 128 // 4) + 1, jnp.int32)
        _ctx_2048P = jax.random.normal(jax.random.fold_in(_rk, 11), (16, 16, 256), jnp.float32)
        _ctx_2048c = jax.random.dirichlet(jax.random.fold_in(_rk, 511), 0.3 * jnp.ones((16,), jnp.float32), (16, 128))
        _ctx_2048t = jnp.einsum('bsk,bkd->bsd', _ctx_2048c, _ctx_2048P)
        _ctx_2048t = _ctx_2048t * jax.lax.rsqrt(jnp.mean(jnp.square(_ctx_2048t)) + 1e-12) * 0.953939
        ctx_2048 = -1.52775e-05 + 0.999936 * (_ctx_2048t + 0.3 * jax.random.normal(jax.random.fold_in(_rk, 611), (16, 128, 256), jnp.float32))
        return (x, ctx_2048)
    x, ctx_2048 = _rec_inputs()

    def _L0_attn_setup():
        import jax, jax.numpy as jnp
        import numpy as np
        DECAY_CONSTANT = 1.0

        def _build_decay_matrices(weight, decay_value, S, dtype):
            i = jnp.arange(S)[:, None]
            j = jnp.arange(S)[None, :]
            mask = j >= i
            e = jnp.where(mask, (j - i).astype(dtype), jnp.asarray(0.0, dtype))
            dv0 = jnp.clip(decay_value[0, 0], 0.9, 1.0).astype(dtype)
            dv1 = jnp.clip(decay_value[1, 0], 0.9, 1.0).astype(dtype)
            w0 = weight[0].astype(dtype)
            w1 = weight[1].astype(dtype)
            Wr = jnp.where(mask, w0[:, None] * (dv0 ** e / DECAY_CONSTANT), jnp.asarray(0.0, dtype))
            Wc = jnp.where(mask, w1[None, :] * dv1 ** (e / DECAY_CONSTANT), jnp.asarray(0.0, dtype))
            return (Wr, Wc)
        key = jax.random.key(seed)
        kx, kw = jax.random.split(key)
        B, E, S = (4, 256, 256)
        x = jax.random.normal(kx, (B, E, S), dtype=jnp.float32)
        weight = jax.random.normal(kw, (2, S), dtype=jnp.float32)
        bias = jnp.zeros((S,), dtype=jnp.float32)
        decay_value = jnp.ones((2, 1), dtype=jnp.float32)
        return {'x': x, 'weight': weight, 'bias': bias, 'decay_value': decay_value}
    _L0_attn_all = _L0_attn_setup()
    _L0_attn_in = {k: v for k, v in _L0_attn_all.items() if k in ('weight', 'bias', 'decay_value')}
    del _L0_attn_all

    def _L0_xattn_setup():
        import jax, jax.numpy as jnp
        import numpy as np
        NUM_HEADS = 16
        key = jax.random.key(seed)
        k1, k2, k3 = jax.random.split(key, 3)
        B, S, D = (4, 512, 256)
        q = jax.random.normal(k1, (B, S, D), dtype=jnp.float32)
        k = jax.random.normal(k2, (B, S, D), dtype=jnp.float32)
        v = jax.random.normal(k3, (B, S, D), dtype=jnp.float32)
        decay = jnp.full((1, NUM_HEADS, 1), 0.9, dtype=jnp.float32)
        return {'q': q, 'k': k, 'v': v, 'decay': decay}
    _L0_xattn_all = _L0_xattn_setup()
    _L0_xattn_in = {k: v for k, v in _L0_xattn_all.items() if k in ('decay',)}
    del _L0_xattn_all

    def _L0_ffn_setup():
        import jax, jax.numpy as jnp
        import numpy as np
        B, S, D = (2, 256, 256)
        H, HD = (16, 128)
        E, K, I = (16, 6, 176)
        SI = 352
        EPS = 1e-06

        def rmsnorm(x, w):
            v = jnp.mean(jnp.square(x), axis=-1, keepdims=True)
            return x * jax.lax.rsqrt(v + EPS) * w
        key = jax.random.key(seed)
        ks = jax.random.split(key, 14)
        s = 0.02
        return {'hidden_states': jax.random.normal(ks[0], (B, S, D), jnp.float32), 'ln1_w': jnp.ones((D,), jnp.float32), 'ln2_w': jnp.ones((D,), jnp.float32), 'wq': jax.random.normal(ks[1], (D, H * HD), jnp.float32) * s, 'wk': jax.random.normal(ks[2], (D, H * HD), jnp.float32) * s, 'wv': jax.random.normal(ks[3], (D, H * HD), jnp.float32) * s, 'wo': jax.random.normal(ks[4], (H * HD, D), jnp.float32) * s, 'gate_w': jax.random.normal(ks[5], (E, D), jnp.float32) * s, 'eg_w': jax.random.normal(ks[6], (E, I, D), jnp.float32) * s, 'eu_w': jax.random.normal(ks[7], (E, I, D), jnp.float32) * s, 'ed_w': jax.random.normal(ks[8], (E, D, I), jnp.float32) * s, 'sg_w': jax.random.normal(ks[9], (SI, D), jnp.float32) * s, 'su_w': jax.random.normal(ks[10], (SI, D), jnp.float32) * s, 'sd_w': jax.random.normal(ks[11], (D, SI), jnp.float32) * s}
    _L0_ffn_all = _L0_ffn_setup()
    _L0_ffn_in = {k: v for k, v in _L0_ffn_all.items() if k in ('ln1_w', 'ln2_w', 'wq', 'wk', 'wv', 'wo', 'gate_w', 'eg_w', 'eu_w', 'ed_w', 'sg_w', 'su_w', 'sd_w')}
    del _L0_ffn_all
    return {'x': x, 'ctx_2048': ctx_2048, 'L0_attn_weight': _L0_attn_in['weight'], 'L0_attn_bias': _L0_attn_in['bias'], 'L0_attn_decay_value': _L0_attn_in['decay_value'], 'L0_xattn_decay': _L0_xattn_in['decay'], 'L0_ffn_ln1_w': _L0_ffn_in['ln1_w'], 'L0_ffn_ln2_w': _L0_ffn_in['ln2_w'], 'L0_ffn_wq': _L0_ffn_in['wq'], 'L0_ffn_wk': _L0_ffn_in['wk'], 'L0_ffn_wv': _L0_ffn_in['wv'], 'L0_ffn_wo': _L0_ffn_in['wo'], 'L0_ffn_gate_w': _L0_ffn_in['gate_w'], 'L0_ffn_eg_w': _L0_ffn_in['eg_w'], 'L0_ffn_eu_w': _L0_ffn_in['eu_w'], 'L0_ffn_ed_w': _L0_ffn_in['ed_w'], 'L0_ffn_sg_w': _L0_ffn_in['sg_w'], 'L0_ffn_su_w': _L0_ffn_in['su_w'], 'L0_ffn_sd_w': _L0_ffn_in['sd_w']}

def reference(x, ctx_2048, L0_attn_weight, L0_attn_bias, L0_attn_decay_value, L0_xattn_decay, L0_ffn_ln1_w, L0_ffn_ln2_w, L0_ffn_wq, L0_ffn_wk, L0_ffn_wv, L0_ffn_wo, L0_ffn_gate_w, L0_ffn_eg_w, L0_ffn_eu_w, L0_ffn_ed_w, L0_ffn_sg_w, L0_ffn_su_w, L0_ffn_sd_w):
    import jax
    import jax.numpy as jnp

    def _L0_attn_ref(x, weight, bias, decay_value):
        import jax, jax.numpy as jnp
        import numpy as np
        DECAY_CONSTANT = 1.0

        def _build_decay_matrices(weight, decay_value, S, dtype):
            i = jnp.arange(S)[:, None]
            j = jnp.arange(S)[None, :]
            mask = j >= i
            e = jnp.where(mask, (j - i).astype(dtype), jnp.asarray(0.0, dtype))
            dv0 = jnp.clip(decay_value[0, 0], 0.9, 1.0).astype(dtype)
            dv1 = jnp.clip(decay_value[1, 0], 0.9, 1.0).astype(dtype)
            w0 = weight[0].astype(dtype)
            w1 = weight[1].astype(dtype)
            Wr = jnp.where(mask, w0[:, None] * (dv0 ** e / DECAY_CONSTANT), jnp.asarray(0.0, dtype))
            Wc = jnp.where(mask, w1[None, :] * dv1 ** (e / DECAY_CONSTANT), jnp.asarray(0.0, dtype))
            return (Wr, Wc)
        B, E, S = x.shape
        Wr, Wc = _build_decay_matrices(weight, decay_value, S, x.dtype)
        out = jnp.einsum('bes,st->bet', x, Wr + Wc)
        out = out + bias.astype(x.dtype)
        return out

    def _L0_xattn_ref(q, k, v, decay):
        import jax, jax.numpy as jnp
        import numpy as np
        NUM_HEADS = 16
        B, S, D = q.shape
        H = NUM_HEADS
        hd = D // H
        qh = q.reshape(B, S, H, hd)
        kh = k.reshape(B, S, H, hd)
        vh = v.reshape(B, S, H, hd)
        kv = kh * vh
        kv_t = jnp.moveaxis(kv, 1, 0)
        d = decay

        def step(r, inc):
            r = d * r + inc
            return (r, r)
        r0 = jnp.zeros((B, H, hd), dtype=q.dtype)
        _, rs = jax.lax.scan(step, r0, kv_t)
        out = qh * jnp.moveaxis(rs, 0, 1)
        return out.reshape(B, S, D)

    def _L0_ffn_ref(hidden_states, ln1_w, ln2_w, wq, wk, wv, wo, gate_w, eg_w, eu_w, ed_w, sg_w, su_w, sd_w):
        import jax, jax.numpy as jnp
        import numpy as np
        B, S, D = (2, 256, 256)
        H, HD = (16, 128)
        E, K, I = (16, 6, 176)
        SI = 352
        EPS = 1e-06

        def rmsnorm(x, w):
            v = jnp.mean(jnp.square(x), axis=-1, keepdims=True)
            return x * jax.lax.rsqrt(v + EPS) * w
        b, s, d = hidden_states.shape
        x = hidden_states
        h = rmsnorm(x, ln1_w)
        q = (h @ wq).reshape(b, s, H, HD)
        k = (h @ wk).reshape(b, s, H, HD)
        v = (h @ wv).reshape(b, s, H, HD)
        scores = jnp.einsum('bqhd,bkhd->bhqk', q, k) / np.sqrt(HD).astype(np.float32)
        causal = jnp.tril(jnp.ones((s, s), bool))
        scores = jnp.where(causal, scores, jnp.float32(-1000000000.0))
        attn = jax.nn.softmax(scores, axis=-1)
        ao = jnp.einsum('bhqk,bkhd->bqhd', attn, v).reshape(b, s, H * HD) @ wo
        x = x + ao
        h = rmsnorm(x, ln2_w)
        t = h.reshape(-1, d)
        T = t.shape[0]
        logits = t @ gate_w.T
        probs = jax.nn.softmax(logits, axis=-1)
        topv, topi = jax.lax.top_k(probs, K)
        topv = topv / jnp.sum(topv, axis=-1, keepdims=True)
        cw = jnp.zeros((T, E), t.dtype).at[jnp.arange(T)[:, None], topi].add(topv)
        g = jnp.einsum('td,eid->eti', t, eg_w)
        u = jnp.einsum('td,eid->eti', t, eu_w)
        hh = jax.nn.silu(g) * u
        routed = jnp.einsum('eti,edi,te->td', hh, ed_w, cw)
        shared = jax.nn.silu(t @ sg_w.T) * (t @ su_w.T) @ sd_w.T
        out = x + (routed + shared).reshape(b, s, d)
        return out
    x = _layernorm(x + _L0_attn_ref(x, L0_attn_weight, L0_attn_bias, L0_attn_decay_value), axis=-1)
    x = _layernorm(x + _L0_xattn_ref(x, ctx_2048, ctx_2048, L0_xattn_decay), axis=-1)
    x = _layernorm(x + _L0_ffn_ref(x, L0_ffn_ln1_w, L0_ffn_ln2_w, L0_ffn_wq, L0_ffn_wk, L0_ffn_wv, L0_ffn_wo, L0_ffn_gate_w, L0_ffn_eg_w, L0_ffn_eu_w, L0_ffn_ed_w, L0_ffn_sg_w, L0_ffn_su_w, L0_ffn_sd_w), axis=-1)
    return x

_drawn_inputs = setup_inputs


def setup_inputs(seed=0):
    import zlib

    import numpy as np

    out = dict(_drawn_inputs(seed))
    spreads = {'L0_attn_bias': (0.0, 0.1),
     'L0_attn_decay_value': (1.0, 0.2),
     'L0_xattn_decay': (0.8999999761581421, 0.2),
     'L0_ffn_ln1_w': (1.0, 0.6),
     'L0_ffn_ln2_w': (1.0, 0.6)}
    factors = {'L0_ffn_wq': 8.0,
     'L0_ffn_wk': 8.0,
     'L0_ffn_gate_w': 8.0,
     'L0_ffn_eg_w': 8.0,
     'L0_ffn_eu_w': 8.0,
     'L0_ffn_ed_w': 8.0,
     'L0_ffn_sg_w': 5.084,
     'L0_ffn_su_w': 5.005,
     'L0_ffn_sd_w': 4.924}
    for name, (base, spread) in spreads.items():
        noise = np.random.default_rng([zlib.crc32(name.encode()), seed]).standard_normal(out[name].shape)
        drawn = base * np.exp(spread * noise) if base else spread * noise
        out[name] = jnp.asarray(drawn.astype(out[name].dtype))
    for name, factor in factors.items():
        out[name] = (out[name] * factor).astype(out[name].dtype)
    return out
```

```python
from contextlib import ExitStack

import concourse.bass as bass
from concourse import mybir

F32 = mybir.dt.float32
F32R = mybir.dt.float32r
ALU = mybir.AluOpType
ACT = mybir.ActivationFunctionType

P = 128
B, S, D = 16, 128, 256
NT = B * S // P
G = 4
TG = NT // G
N = TG * P
KD = D // P
H, HD = 16, 128
PAIRS = H // 2
STEPS = 2 * G
E, TOPK, I, SI = 16, 6, 176, 352
CT = -(-(E * I + SI) // P)
JB = 5
BODIES = CT // JB
MSTEPS = G * JB
WT = 2 * KD * P + D + P
WSPLIT = WT - P
SELP = 64
LN_EPS = 1e-5
RMS_EPS = 1e-6
SCALE = 1.0 / float(HD) ** 0.5
LOWEST = -3.0e38
assert NT == B and H % 2 == 0 and CT == JB * BODIES and KD == 2

PRODUCTS = ((0, 0), (0, 1), (1, 0))


def decoder_layer(nc, x, xT, ctxT, bands, ident_in, mask_in, aw, bias, decay, columns, w_att, gateT, w_moe, out):
    with ExitStack() as ctx:
        def sb(name, shape, dt=F32, at=ctx):
            return at.enter_context(nc.sbuf_tensor(name, shape, dt))

        def sem(name):
            return ctx.enter_context(nc.semaphore(name))

        bank = [ctx.enter_context(nc.psum_tensor(f"bank{n}", [P, N], F32)) for n in range(8)]

        xs = sb("xs", [P, NT, D])
        x2 = sb("x2", [P, NT, D])
        xn = sb("xn", [P, NT, D])
        hT = [sb("hT_hi", [P, KD, NT * P], F32R), sb("hT_lo", [P, KD, NT * P], F32R)]
        ident = sb("ident", [P, P])
        mask = sb("mask", [P, P])
        vec = sb("vec", [P, 4, KD])
        w0_col, xdec, lnw = vec[:, 0, :], vec[:, 1, :], vec[:, 2:4, :]
        stats = sb("stats", [P, NT, 6])
        mv = sb("mv", [P, NT, 2])
        ssq = sb("ssq", [P, NT])
        std = sb("std", [P, NT])
        rstd = sb("rstd", [P, NT])
        pause = sb("pause", [P, 16])
        raw_qk = sb("raw_qk", [P, 2, 2, KD, HD])
        raw_v = sb("raw_v", [P, KD, 2 * HD])
        raw_o = sb("raw_o", [P, 2, D])
        w_qk = [sb("w_qk_hi", [P, 2, 2, KD, HD], F32R), sb("w_qk_lo", [P, 2, 2, KD, HD], F32R)]
        w_v = [sb("w_v_hi", [P, KD, 2 * HD], F32R), sb("w_v_lo", [P, KD, 2 * HD], F32R)]
        w_o = [sb("w_o_hi", [P, 2, D], F32R), sb("w_o_lo", [P, 2, D], F32R)]
        raw_m = sb("raw_m", [P, JB, WT])

        with ExitStack() as first:
            xT_sb = sb("xT_sb", [P, KD, NT * P], at=first)
            ctx_sb = sb("ctx_sb", [P, KD, NT * P], at=first)
            run_sb = sb("run_sb", [P, KD, NT * P], at=first)
            band = sb("band", [P, KD, D], at=first)
            pow0 = sb("pow0", [P, KD, D], at=first)
            pow1 = sb("pow1", [P, KD, D], at=first)
            wsum = sb("wsum", [P, KD, D], at=first)
            w1_row = sb("w1_row", [P, D], at=first)
            bias_row = sb("bias_row", [P, D], at=first)
            dv = sb("dv", [P, 2], at=first)
        with ExitStack() as second:
            v_sb = sb("v_sb", [P, NT, 2 * HD], at=second)
            qT = sb("qT", [P, N], at=second)
            kT = sb("kT", [P, N], at=second)
            pT = sb("pT", [P, N], at=second)
            oT = [sb("oT_hi", [P, G + 1, N], F32R, second), sb("oT_lo", [P, G + 1, N], F32R, second)]
            prob = sb("prob", [P, TG, S], at=second)
            rowmax = sb("rowmax", [P, TG], at=second)
            nbias = sb("nbias", [P, TG], at=second)
            rowsum = sb("rowsum", [P, TG], at=second)
            rinv = sb("rinv", [P, TG], at=second)
        with ExitStack() as third:
            wm = [sb("wm_hi", [P, JB, WT], F32R, third), sb("wm_lo", [P, JB, WSPLIT], F32R, third)]
            gate_raw = sb("gate_raw", [P, KD, E], at=third)
            gate_w = [sb("gate_hi", [P, KD, E], F32R, third), sb("gate_lo", [P, KD, E], F32R, third)]
            logit = sb("logit", [P, NT, E], at=third)
            lmax = sb("lmax", [P, NT], at=third)
            lsum = sb("lsum", [P, NT], at=third)
            best = sb("best", [P, NT, 8], at=third)
            rest = sb("rest", [P, NT, E], at=third)
            cw = sb("cw", [P, NT, E], at=third)
            cw_hi = sb("cw_hi", [P, NT, E], F32R, third)
            cw_rows = sb("cw_rows", [P, NT, SELP], at=third)
            cwT = sb("cwT", [SELP, NT * P], F32R, third)
            silu = sb("silu", [P, 2, N], at=third)
            gated = sb("gated", [P, 2, N], at=third)
            hid = sb("hid", [P, 2, N], at=third)
            hh = [sb("hh_hi", [P, 2, N], F32R, third), sb("hh_lo", [P, 2, N], F32R, third)]

        Q_PS, K_PS, VO_PS, S_PS, PT_PS, O_PS = bank[0], bank[1], bank[2:4], bank[4], bank[5], bank[6]
        G_PS, U_PS, CW_PS, ACC_PS = bank[0:2], bank[2:4], bank[4:6], bank[6:8]

        ld_small, ld_xT, ld_x, ld_ctx = sem("ld_small"), sem("ld_xT"), sem("ld_x"), sem("ld_ctx")
        ld_qk = [sem("ld_qk0"), sem("ld_qk1")]
        ld_v, ld_o, ld_moe, ld_gate = sem("ld_v"), sem("ld_o"), sem("ld_moe"), sem("ld_gate")
        stored = sem("stored")
        dve_chain, act_chain, pool_chain = sem("dve_chain"), sem("act_chain"), sem("pool_chain")
        ctx_sq, w_ready, x_bias, xw_done, x_added = (sem(n) for n in ("ctx_sq", "w_ready", "x_bias", "xw_done", "x_added"))
        run_ready, run_T, x_scanned = sem("run_ready"), sem("run_T"), sem("x_scanned")
        var_ready, std_ready, ssq_ready = sem("var_ready"), sem("std_ready"), sem("ssq_ready")
        x_normed, xn_ready, xn_T, h_hi, h_lo = (sem(n) for n in ("x_normed", "xn_ready", "xn_T", "h_hi", "h_lo"))
        zeroed = sem("zeroed")
        q_done, k_done, s_done, pt_done, o_done, v_done, wo_done = (
            sem(n) for n in ("q_done", "k_done", "s_done", "pt_done", "o_done", "v_done", "wo_done"))
        q_sbuf, k_sbuf, pt_sbuf, v_sbuf = (sem(n) for n in ("q_sbuf", "k_sbuf", "pt_sbuf", "v_sbuf"))
        o_hi, o_lo = sem("o_hi"), sem("o_lo")
        masked, nbias_ready, exp_done, rinv_ready, prob_ready, wo_added = (
            sem(n) for n in ("masked", "nbias_ready", "exp_done", "rinv_ready", "prob_ready", "wo_added"))
        w_hi_ready, qk_ready, v_ready, o_ready = sem("w_hi_ready"), [sem("qk0_ready"), sem("qk1_ready")], sem("v_ready"), sem("o_ready")
        gate_split, logit_done, cw_ready, cw_T, cwT_ready = (
            sem(n) for n in ("gate_split", "logit_done", "cw_ready", "cw_T", "cwT_ready"))
        wm_hi_ready, wm_ready = sem("wm_hi_ready"), sem("wm_ready")
        g_done, u_done, c_done, d_done, acc_zero = (sem(n) for n in ("g_done", "u_done", "c_done", "d_done", "acc_zero"))
        silu_ready, gated_ready, hid_ready, hh_hi, hh_lo, acc_added = (
            sem(n) for n in ("silu_ready", "gated_ready", "hid_ready", "hh_hi", "hh_lo", "acc_added"))
        final_ready, x_copied = sem("final_ready"), sem("x_copied")

        def group_of(n):
            return slice(n * N, (n + 1) * N)

        def cols(n, w=P):
            return slice(n * w, (n + 1) * w)

        def row_bcast(ap, n):
            return ap.rearrange("(o n) -> o n", o=1).to_broadcast([P, n])

        def qk_parts(head):
            return raw_qk[:, head], [w[:, head] for w in w_qk]

        def v_parts():
            return raw_v[:], [w[:] for w in w_v]

        def o_parts():
            return raw_o[:], [w[:] for w in w_o]

        block = ctx.enter_context(nc.Block())

        @block.sync
        def _(sp):
            sp.dma_start(band[:], bands).then_inc(ld_small, 16)
            sp.dma_start(w1_row[:], row_bcast(aw[1], D)).then_inc(ld_small, 16)
            sp.dma_start(bias_row[:], row_bcast(bias, D)).then_inc(ld_small, 16)
            sp.dma_start(dv[:], row_bcast(decay, 2)).then_inc(ld_small, 16)
            sp.dma_start(vec[:], columns).then_inc(ld_small, 16)
            sp.dma_start(ident[:], ident_in).then_inc(ld_small, 16)
            sp.dma_start(mask[:], mask_in).then_inc(ld_small, 16)
            sp.dma_start(xT_sb[:], xT.rearrange("(c p) t -> p c t", p=P)).then_inc(ld_xT, 16)
            sp.dma_start(ctx_sb[:], ctxT.rearrange("(c p) t -> p c t", p=P)).then_inc(ld_ctx, 16)
            sp.dma_start(xs[:], x.rearrange("t p d -> p t d")).then_inc(ld_x, 16)

            def load_qk(pair, head):
                sp.dma_start(raw_qk[:, head], w_att[pair, :, cols(head, 2 * KD * HD)].rearrange(
                    "p (a c n) -> p a c n", a=2, c=KD)).then_inc(ld_qk[head], 16)

            def load_v(pair):
                sp.dma_start(raw_v[:], w_att[pair, :, cols(2, 2 * KD * HD)].rearrange(
                    "p (c n) -> p c n", c=KD)).then_inc(ld_v, 16)

            def load_o(pair):
                sp.dma_start(raw_o[:], w_att[pair, :, cols(3, 2 * D)].rearrange(
                    "p (a n) -> p a n", a=2)).then_inc(ld_o, 16)

            load_qk(0, 0)
            load_v(0)
            load_qk(0, 1)
            load_o(0)
            with sp.Fori(0, PAIRS) as i:
                sp.wait_ge(qk_ready[0], i + 1)
                load_qk(i + 1, 0)
                sp.wait_ge(v_ready, i + 1)
                load_v(i + 1)
                sp.wait_ge(qk_ready[1], i + 1)
                load_qk(i + 1, 1)
                sp.wait_ge(o_ready, i + 1)
                load_o(i + 1)
            sp.dma_start(raw_m[:], w_moe[0]).then_inc(ld_moe, 16)
            sp.wait_ge(wo_added, 2 * G * PAIRS + 5)
            sp.wait_ge(o_lo, STEPS * PAIRS + 3)
            sp.dma_start(gate_raw[:], gateT).then_inc(ld_gate, 16)
            with sp.Fori(1, BODIES + 1) as i:
                sp.wait_ge(wm_ready, i * JB)
                sp.dma_start(raw_m[:], w_moe[i]).then_inc(ld_moe, 16)
            for t in range(0, NT, TG):
                sp.wait_ge(final_ready, t + TG)
                sp.dma_start(out[t:t + TG].rearrange("t p d -> p t d"), xn[:, t:t + TG]).then_inc(stored, 16)
            sp.wait_ge(stored, 16 * G)

        @block.tensor
        def _(pe):
            def split_matmul(out_ap, pairs, first=True, last=True, **kw):
                n, total = 0, len(pairs) * len(PRODUCTS)
                for stat, mov in pairs:
                    for a, b in PRODUCTS:
                        mm = nc.tensor.matmul(out_ap, stat(a), mov(b), start=first and n == 0,
                                              stop=last and n == total - 1, **kw)
                        n += 1
                return mm

            pe.wait_ge(ld_xT, 16)
            pe.wait_ge(w_ready, KD)
            for t in range(NT):
                for c in range(KD):
                    mm = nc.tensor.matmul(bank[t // 2][:, cols(t % 2, D)], xT_sb[:, c, cols(t)], wsum[:, c, :],
                                          start=c == 0, stop=c == KD - 1)
                if t % 2:
                    mm.then_inc(xw_done, 1)
            pe.wait_ge(ld_small, 16 * 7)
            for t in range(NT):
                if t % 2 == 0:
                    pe.wait_ge(run_ready, t + 2)
                    pe.wait_ge(x_added, t // 2 + 1)
                for c in range(KD):
                    mm = nc.tensor.transpose(bank[t // 2][:, D * (t % 2) + P * c:D * (t % 2) + P * (c + 1)],
                                             run_sb[:, c, cols(t)], ident[:])
                if t % 2:
                    mm.then_inc(run_T, 1)

            def transpose_normed(times):
                for g in range(G):
                    pe.wait_ge(xn_ready, (times - 1) * NT + TG * (g + 1))
                    for c in range(KD):
                        for b in range(TG):
                            mm = nc.tensor.transpose(bank[KD * g + c][:, cols(b)], xn[:, TG * g + b, cols(c)], ident[:])
                        mm.then_inc(xn_T, 1)

            transpose_normed(1)

            def project(n, j, which, ps, done, copied):
                head, g = j // G, j % G
                pe.wait_ge(copied, n + 1)
                split_matmul(ps[:], [(lambda a, c=c: w_qk[a][:, head, which, c, :],
                                      lambda b, c=c: hT[b][:, c, group_of(g)]) for c in range(KD)]).then_inc(done, 1)

            def weighted_values(n, j):
                head, g = j // G, j % G
                pe.wait_ge(pt_sbuf, n + 3)
                pe.wait_ge(o_lo, n + 3)
                for b in range(TG):
                    mm = nc.tensor.matmul(O_PS[:, cols(b)], v_sb[:, TG * g + b, cols(head)], pT[:, cols(b)],
                                          start=True, stop=True)
                mm.then_inc(o_done, 1)

            def transpose_probs(n):
                pe.wait_ge(prob_ready, n + 2)
                for b in range(TG):
                    mm = nc.tensor.transpose(PT_PS[:, cols(b)], prob[:, b, :], ident[:])
                mm.then_inc(pt_done, 1)

            def values(i, g):
                for half in range(2):
                    if g:
                        pe.wait_ge(v_sbuf, i * 2 * G + 2 * (g - 1) + half + 1)
                    else:
                        pe.wait_ge(wo_added, i * 2 * G + 2 + half + 2)
                    for b in range(2):
                        t = TG * g + 2 * half + b
                        mm = split_matmul(VO_PS[half][:, cols(b, D)],
                                          [(lambda a, c=c: hT[a][:, c, cols(t)], lambda m, c=c: w_v[m][:, c, :])
                                           for c in range(KD)])
                    mm.then_inc(v_done, 1)

            def project_out(i, m):
                g = (m + 2) % G
                for half in range(2):
                    if m == 2:
                        pe.wait_ge(v_sbuf, i * 2 * G + 2 * (G - 1) + half + 1)
                    elif m == 0:
                        pe.wait_ge(wo_added, i * 2 * G + 1)
                    else:
                        pe.wait_ge(wo_added, i * 2 * G + 2 * (m - 1) + half + 2)
                    for b in range(2):
                        t = 2 * half + b
                        mm = split_matmul(VO_PS[half][:, cols(b, D)],
                                          [(lambda a, h=h: oT[a][:, G if h else g, cols(t)], lambda w, h=h: w_o[w][:, h, :])
                                           for h in range(2)])
                    mm.then_inc(wo_done, 1)

            pe.wait_ge(h_lo, G * KD)
            pe.wait_ge(zeroed, 6)
            for b in range(TG):
                mm = nc.tensor.transpose(PT_PS[:, cols(b)], prob[:, b, :], ident[:])
            mm.then_inc(pt_done, 1)
            nc.tensor.matmul(S_PS[:], prob[:, 0, :], xn[:, 0:2, :], start=True, stop=True).then_inc(s_done, 1)
            with pe.Fori(0, PAIRS) as i:
                for j in range(STEPS):
                    n = i * STEPS + j
                    if j % G == 0:
                        pe.wait_ge(qk_ready[j // G], i + 1)
                    project(n, j, 0, Q_PS, q_done, q_sbuf)
                    if 2 <= j < 2 + G:
                        pe.wait_ge(v_sbuf, i * 2 * G + 2 * (j - 1))
                    weighted_values(n - 2, (j - 2) % STEPS)
                    project(n, j, 1, K_PS, k_done, k_sbuf)
                    if j == 0:
                        pe.wait_ge(o_lo, n + 2)
                        project_out(i, 0)
                    if j == 1:
                        pe.wait_ge(o_lo, n + 2)
                        project_out(i, 1)
                        pe.wait_ge(v_ready, i + 1)
                    if 1 <= j <= G:
                        values(i, j - 1)
                    if j == 6:
                        pe.wait_ge(o_ready, i + 1)
                    if j >= 6:
                        pe.wait_ge(o_lo, n + 2)
                        project_out(i, j - 4)
                    transpose_probs(n - 1)
                    pe.wait_ge(q_sbuf, n + 2)
                    pe.wait_ge(k_sbuf, n + 2)
                    for b in range(TG):
                        mm = nc.tensor.matmul(S_PS[:, cols(b)], qT[:, cols(b)], kT[:, cols(b)], start=True, stop=True)
                    mm.then_inc(s_done, 1)
            last = PAIRS * STEPS
            weighted_values(last - 2, STEPS - 2)
            transpose_probs(last - 1)
            pe.wait_ge(o_lo, last + 2)
            project_out(PAIRS, 0)
            weighted_values(last - 1, STEPS - 1)
            pe.wait_ge(o_lo, last + 3)
            project_out(PAIRS, 1)

            transpose_normed(2)
            pe.wait_ge(gate_split, 2)
            pe.wait_ge(h_lo, 2 * G * KD)
            for t in range(NT):
                mm = split_matmul(bank[0][:, cols(t, E)], [(lambda a, c=c: hT[a][:, c, cols(t)],
                                                            lambda m, c=c: gate_w[m][:, c, :]) for c in range(KD)])
            mm.then_inc(logit_done, 1)
            pe.wait_ge(cw_ready, 1)
            for g in range(G):
                for b in range(TG):
                    mm = nc.tensor.transpose(CW_PS[g % 2][0:SELP, cols(b)] if g < 2 else U_PS[g % 2][0:SELP, cols(b)],
                                             cw_rows[:, TG * g + b, :], ident[:])
                mm.then_inc(cw_T, 1)

            def down(n, j, par):
                pe.wait_ge(hh_lo, n + 2)
                for half in range(2):
                    for b in range(2):
                        t = 2 * half + b
                        mm = split_matmul(ACC_PS[half][:, cols(b, D)],
                                          [(lambda a: hh[a][:, par, cols(t)],
                                            lambda m: wm[m][:, j, 2 * KD * P:2 * KD * P + D])],
                                          first=j == 0 and b == 0, last=j == JB - 1, skip_group_check=True)
                mm.then_inc(d_done, 1)

            pe.wait_ge(cwT_ready, G)
            pe.wait_ge(hh_lo, 1)
            for half in range(2):
                mm = nc.tensor.matmul(ACC_PS[half][:], hh[0][:, 1, 0:P], hh[0][:, 1, :], start=True, stop=False,
                                      skip_group_check=True)
            with pe.Fori(0, BODIES) as i:
                for s in range(MSTEPS):
                    g, j, par = s // JB, s % JB, s % 2
                    n = i * MSTEPS + s
                    if g == 0:
                        pe.wait_ge(wm_ready, i * JB + j + 1)
                    pe.wait_ge(silu_ready, n + 1)
                    split_matmul(G_PS[par][:], [(lambda a, c=c: wm[a][:, j, cols(c)],
                                                 lambda m, c=c: hT[m][:, c, group_of(g)]) for c in range(KD)]).then_inc(g_done, 1)
                    pe.wait_ge(hid_ready, n + 1)
                    split_matmul(U_PS[par][:], [(lambda a, c=c: wm[a][:, j, cols(KD + c)],
                                                 lambda m, c=c: hT[m][:, c, group_of(g)]) for c in range(KD)]).then_inc(u_done, 1)
                    nc.tensor.matmul(CW_PS[par][:], wm[0][0:SELP, j, WSPLIT:WT], cwT[:, group_of(g)],
                                     start=True, stop=True).then_inc(c_done, 1)
                    if j == 1:
                        pe.wait_ge(acc_added, i * G + g + 1)
                    down(n - 1, (j - 1) % JB, 1 - par)
            down(BODIES * MSTEPS - 1, JB - 1, 1)

        @block.scalar
        def _(act):
            copy, square = ACT.Copy, ACT.Square
            act.wait_ge(ld_ctx, 16)
            for c in range(KD):
                for g in range(G):
                    nc.scalar.activation(ctx_sb[:, c, group_of(g)], ctx_sb[:, c, group_of(g)], square).then_inc(ctx_sq, 1)

            def square_root(times):
                act.wait_ge(var_ready, times)
                nc.scalar.activation(std[:], ssq[:], ACT.Sqrt).then_inc(std_ready, 1)

            def normed_high(times):
                for g in range(G):
                    for c in range(KD):
                        act.wait_ge(xn_T, (times - 1) * G * KD + KD * g + c + 1)
                        nc.scalar.activation(hT[0][:, c, group_of(g)], bank[KD * g + c][:], copy,
                                             scale=lnw[:, times - 1, c:c + 1]).then_inc(h_hi, 1)

            def sum_squares(times, src, after, count):
                act.wait_ge(after, count)
                for t in range(NT):
                    ins = nc.scalar.activation(xn[:, t, :], src[:, t, :], square, accum_out=ssq[:, t:t + 1])
                ins.then_inc(ssq_ready, 1)

            def weights_high(loaded, value, raw, parts):
                act.wait_ge(loaded, value)
                nc.scalar.activation(parts[0], raw, copy).then_inc(w_hi_ready, 1)

            weights_high(ld_qk[0], 16, *qk_parts(0))
            weights_high(ld_v, 16, *v_parts())
            square_root(1)
            square_root(2)
            sum_squares(1, x2, x_normed, 2 * NT)
            square_root(3)
            normed_high(1)

            def outputs_high(n, j):
                act.wait_ge(o_done, n + 3)
                nc.scalar.activation(oT[0][:, j if j < G else G, :], O_PS[:], copy).then_inc(o_hi, 1)

            def exponentials(n):
                act.wait_ge(nbias_ready, n + 2)
                for b in range(TG):
                    ins = nc.scalar.activation(prob[:, b, :], prob[:, b, :], ACT.Exp, bias=nbias[:, b:b + 1],
                                               scale=SCALE, accum_out=rowsum[:, b:b + 1])
                ins.then_inc(exp_done, 1)

            with act.Fori(0, PAIRS) as i:
                for j in range(STEPS):
                    n = i * STEPS + j
                    act.wait_ge(q_done, n + 1)
                    nc.scalar.activation(qT[:], Q_PS[:], copy).then_inc(q_sbuf, 1)
                    outputs_high(n - 2, (j - 2) % STEPS)
                    exponentials(n - 1)
                    if j == 0:
                        act.wait_ge(k_done, n + 1)
                        weights_high(ld_qk[1], i * 16 + 16, *qk_parts(1))
                    if j == 2:
                        act.wait_ge(wo_done, i * 2 * G + 4)
                        weights_high(ld_o, i * 16 + 16, *o_parts())
                    if j == 4:
                        act.wait_ge(k_done, n + 1)
                        weights_high(ld_qk[0], i * 16 + 32, *qk_parts(0))
                    if j == 5:
                        weights_high(ld_v, i * 16 + 32, *v_parts())
                    if 1 <= j <= G:
                        for half in range(2):
                            t = TG * (j - 1) + 2 * half
                            act.wait_ge(v_done, i * 2 * G + 2 * (j - 1) + half + 1)
                            nc.scalar.activation(v_sb[:, t:t + 2, :],
                                                 VO_PS[half][:].rearrange("p (t n) -> p t n", t=2), copy).then_inc(v_sbuf, 1)
            last = PAIRS * STEPS
            outputs_high(last - 2, STEPS - 2)
            exponentials(last - 1)
            outputs_high(last - 1, STEPS - 1)

            sum_squares(2, xs, wo_added, 2 * G * PAIRS + 5)
            square_root(4)
            normed_high(2)
            act.wait_ge(ld_gate, 16)
            nc.scalar.activation(gate_w[0][:], gate_raw[:], copy).then_inc(gate_split, 1)
            act.wait_ge(var_ready, 5)
            nc.scalar.activation(logit[:], logit[:], ACT.Exp).then_inc(std_ready, 1)
            for g in range(G):
                act.wait_ge(cw_T, g + 1)
                nc.scalar.activation(cwT[:, group_of(g)], (CW_PS if g < 2 else U_PS)[g % 2][0:SELP, :], copy).then_inc(cwT_ready, 1)

            def expert_weights_high(body, j):
                act.wait_ge(ld_moe, body * 16 + 16)
                nc.scalar.activation(wm[0][:, j, :], raw_m[:, j, :], copy).then_inc(wm_hi_ready, 1)

            def hidden_high(n, par):
                act.wait_ge(hid_ready, n + 3)
                nc.scalar.activation(hh[0][:, par, :], hid[:, par, :], copy).then_inc(hh_hi, 1)

            act.wait_ge(zeroed, 11)
            for j in range(JB - 1):
                expert_weights_high(0, j)
            with act.Fori(0, BODIES) as i:
                for s in range(MSTEPS):
                    g, j, par = s // JB, s % JB, s % 2
                    n = i * MSTEPS + s
                    act.wait_ge(g_done, n + 1)
                    act.wait_ge(gated_ready, n + 1)
                    nc.scalar.activation(silu[:, par, :], G_PS[par][:], ACT.Silu).then_inc(silu_ready, 1)
                    hidden_high(n, par)
                    if s == 0:
                        act.wait_ge(d_done, n + 1)
                        expert_weights_high(i, JB - 1)
                    if s > MSTEPS - JB:
                        act.wait_ge(d_done, n + 1)
                        expert_weights_high(i + 1, j - 1)
            square_root(6)

        @block.gpsimd
        def _(pool):
            def weights_low(value, raw, parts, ready):
                pool.wait_ge(w_hi_ready, value)
                nc.gpsimd.tensor_tensor(parts[1], raw, parts[0].bitcast(F32), ALU.subtract).then_inc(ready, 1)

            pool.wait_ge(ld_x, 16)
            pool.wait_ge(ld_small, 16 * 7)
            for t in range(0, NT, 2):
                nc.gpsimd.tensor_tensor(xs[:, t:t + 2, :], xs[:, t:t + 2, :],
                                        bias_row[:].rearrange("p (o n) -> p o n", o=1).to_broadcast([P, 2, D]),
                                        ALU.add).then_inc(x_bias, 1)
            weights_low(1, *qk_parts(0), qk_ready[0])
            weights_low(2, *v_parts(), v_ready)
            nc.gpsimd.memset(w_o[0][:].bitcast(F32), 0.0).then_inc(zeroed, 1)
            nc.gpsimd.memset(w_o[1][:].bitcast(F32), 0.0).then_inc(zeroed, 1)
            pool.wait_ge(run_T, NT // 2)
            for part in range(2):
                nc.gpsimd.memset(oT[part][:, 2:4, :].bitcast(F32), 0.0).then_inc(zeroed, 1)
            nc.gpsimd.memset(v_sb[:, NT // 2:NT, :], 0.0).then_inc(zeroed, 1)
            nc.gpsimd.memset(prob[:], 0.0).then_inc(zeroed, 1)

            for t in range(0, NT, 2):
                pool.wait_ge(x_normed, NT + t + 2)
                nc.gpsimd.tensor_copy(xs[:, t:t + 2, :], x2[:, t:t + 2, :]).then_inc(x_copied, 1)

            def normalise(n):
                pool.wait_ge(rinv_ready, n + 2)
                nc.gpsimd.tensor_tensor(prob[:], prob[:], rinv[:].rearrange("p (b o) -> p b o", o=1).to_broadcast([P, TG, S]),
                                        ALU.mult).then_inc(prob_ready, 1)

            with pool.Fori(0, PAIRS) as i:
                for j in range(STEPS):
                    n = i * STEPS + j
                    normalise(n - 1)
                    if j == 0:
                        weights_low(4 * i + 3, *qk_parts(1), qk_ready[1])
                    if j == 2:
                        weights_low(4 * i + 4, *o_parts(), o_ready)
                    if j == 4:
                        weights_low(4 * i + 5, *qk_parts(0), qk_ready[0])
                    if j == 5:
                        weights_low(4 * i + 6, *v_parts(), v_ready)
            normalise(PAIRS * STEPS - 1)

            pool.wait_ge(wo_added, 2 * G * PAIRS + 5)
            pool.wait_ge(o_lo, PAIRS * STEPS + 3)
            nc.gpsimd.memset(cw_rows[:], 0.0).then_inc(zeroed, 1)
            for part in range(2):
                nc.gpsimd.memset(hh[part][:, 1, :].bitcast(F32), 0.0).then_inc(zeroed, 1)
                nc.gpsimd.memset(wm[part][:, JB - 1, 2 * KD * P:WSPLIT].bitcast(F32), 0.0).then_inc(zeroed, 1)

            for t in range(0, NT, 2):
                pool.wait_ge(xn_ready, NT + t + 2)
                nc.gpsimd.tensor_tensor(xs[:, t:t + 2, :], xs[:, t:t + 2, :], x2[:, t:t + 2, :],
                                        ALU.add).then_inc(x_copied, 1)

            def expert_weights_low(body, j):
                pool.wait_ge(wm_hi_ready, body * JB + j + 1)
                nc.gpsimd.tensor_tensor(wm[1][:, j, :], raw_m[:, j, 0:WSPLIT], wm[0][:, j, 0:WSPLIT].bitcast(F32),
                                        ALU.subtract).then_inc(wm_ready, 1)

            with pool.Fori(0, BODIES) as i:
                for j in range(JB):
                    expert_weights_low(i, j)

        @block.vector
        def _(dve):
            chain = [0]

            def link(ins):
                chain[0] += 1
                ins.then_inc(dve_chain, 1)
                dve.wait_ge(dve_chain, chain[0])

            dve.wait_ge(ld_small, 16 * 7)
            link(nc.vector.tensor_scalar(dv[:], dv[:], 0.9, 1.0, ALU.max, ALU.min))
            for c in range(KD):
                nc.vector.tensor_tensor_scan(pow0[:, c, :], dv[:, 0:1].to_broadcast([P, D]), band[:, c, :], 0.0, ALU.mult, ALU.add)
                link(nc.vector.tensor_tensor_scan(pow1[:, c, :], dv[:, 1:2].to_broadcast([P, D]), band[:, c, :], 0.0, ALU.mult, ALU.add))
                link(nc.vector.tensor_tensor(pow1[:, c, :], pow1[:, c, :], w1_row[:], ALU.mult))
                nc.vector.scalar_tensor_tensor(wsum[:, c, :], pow0[:, c, :], w0_col[:, c:c + 1], pow1[:, c, :],
                                               ALU.mult, ALU.add).then_inc(w_ready, 1)
            for t in range(NT):
                for c in range(KD):
                    dve.wait_ge(ctx_sq, G * c + t // TG + 1)
                    ins = nc.vector.tensor_tensor_scan(run_sb[:, c, cols(t)], xdec[:, c:c + 1].to_broadcast([P, S]),
                                                       ctx_sb[:, c, cols(t)], 0.0, ALU.mult, ALU.add)
                ins.then_inc(run_ready, 1)

            def inverse_std(times):
                dve.wait_ge(std_ready, times)
                link(nc.vector.reciprocal(rstd[:], std[:]))
                link(nc.vector.tensor_tensor(ssq[:], ssq[:], rstd[:], ALU.mult))
                link(nc.vector.tensor_tensor(ssq[:], ssq[:], rstd[:], ALU.mult))
                link(nc.vector.tensor_scalar(ssq[:], ssq[:], -0.5, 1.5, ALU.mult, ALU.add))
                link(nc.vector.tensor_tensor(rstd[:], rstd[:], ssq[:], ALU.mult))

            def layernorm_stats():
                for t in range(NT):
                    ins = nc.vector.bn_stats(stats[:, t, :], xs[:, t, :])
                link(ins)
                for t in range(NT):
                    ins = nc.vector.bn_aggr(mv[:, t, :], stats[:, t, :])
                link(ins)
                nc.vector.tensor_scalar(ssq[:], mv[:, :, 1], LN_EPS, None, ALU.add).then_inc(var_ready, 1)

            def layernorm(times, dst, done):
                layernorm_stats()
                inverse_std(times)
                for t in range(NT):
                    nc.vector.tensor_scalar(dst[:, t, :], xs[:, t, :], mv[:, t, 0:1], rstd[:, t:t + 1],
                                            ALU.subtract, ALU.mult).then_inc(done, 1)

            def pair_of(ps):
                return ps[:].rearrange("p (t n) -> p t n", t=2)

            for m in range(NT // 2):
                dve.wait_ge(x_bias, m + 1)
                dve.wait_ge(xw_done, m + 1)
                nc.vector.tensor_tensor(xs[:, 2 * m:2 * m + 2, :], pair_of(bank[m]), xs[:, 2 * m:2 * m + 2, :],
                                        ALU.add).then_inc(x_added, 1)
            dve.wait_ge(x_added, NT // 2)
            layernorm(1, xs, x_normed)
            dve.wait_ge(x_normed, NT)
            for m in range(NT // 2):
                dve.wait_ge(run_T, m + 1)
                nc.vector.scalar_tensor_tensor(xs[:, 2 * m:2 * m + 2, :], pair_of(bank[m]), 1.0,
                                               xs[:, 2 * m:2 * m + 2, :], ALU.add, ALU.mult).then_inc(x_scanned, 1)
            dve.wait_ge(x_scanned, NT // 2)
            layernorm(2, x2, x_normed)

            def rms_normalise(times, src, std_count):
                dve.wait_ge(ssq_ready, times)
                nc.vector.tensor_scalar(ssq[:], ssq[:], 1.0 / D, RMS_EPS, ALU.mult, ALU.add).then_inc(var_ready, 1)
                inverse_std(std_count)
                for t in range(NT):
                    nc.vector.tensor_scalar(xn[:, t, :], src[:, t, :], rstd[:, t:t + 1], None, ALU.mult).then_inc(xn_ready, 1)
                for g in range(G):
                    for c in range(KD):
                        dve.wait_ge(h_hi, (times - 1) * G * KD + KD * g + c + 1)
                        nc.vector.scalar_tensor_tensor(hT[1][:, c, group_of(g)], bank[KD * g + c][:],
                                                       lnw[:, times - 1, c:c + 1], hT[0][:, c, group_of(g)].bitcast(F32),
                                                       ALU.mult, ALU.subtract).then_inc(h_lo, 1)

            rms_normalise(1, x2, 3)

            def row_bias(n):
                dve.wait_ge(s_done, n + 2)
                nc.vector.memset(pause[:, 0:1], 0.0)
                for b in range(TG):
                    ins = nc.vector.tensor_tensor_reduce(prob[:, b, :], S_PS[:, cols(b)], mask[:], 1.0, LOWEST,
                                                         ALU.add, ALU.max, accum_out=rowmax[:, b:b + 1])
                ins.then_inc(masked, 1)
                dve.wait_ge(masked, n + 2)
                nc.vector.tensor_scalar(nbias[:], rowmax[:], -SCALE, None, ALU.mult).then_inc(nbias_ready, 1)

            def copy_probs(n):
                dve.wait_ge(pt_done, n + 3)
                nc.vector.tensor_copy(pT[:], PT_PS[:]).then_inc(pt_sbuf, 1)

            def outputs_low(n, j):
                slot = j if j < G else G
                dve.wait_ge(o_hi, n + 3)
                nc.vector.tensor_tensor(oT[1][:, slot, :], O_PS[:], oT[0][:, slot, :].bitcast(F32),
                                        ALU.subtract).then_inc(o_lo, 1)

            def inverse_sum(n):
                dve.wait_ge(exp_done, n + 2)
                nc.vector.reciprocal(rinv[:], rowsum[:]).then_inc(rinv_ready, 1)

            def add_outputs(i, m):
                g = (m + 2) % G
                for half in range(2):
                    t = TG * g + 2 * half
                    dve.wait_ge(wo_done, i * 2 * G + 2 * m + half + 1)
                    nc.vector.tensor_tensor(xs[:, t:t + 2, :], pair_of(VO_PS[half]), xs[:, t:t + 2, :],
                                            ALU.add).then_inc(wo_added, 1)

            dve.wait_ge(x_copied, NT // 2)
            for k, signal in enumerate((q_sbuf, k_sbuf, o_lo, wo_added)):
                nc.vector.memset(pause[:, 8 + k:9 + k], 0.0).then_inc(signal, 1)
            with dve.Fori(0, PAIRS) as i:
                for j in range(STEPS):
                    n = i * STEPS + j
                    copy_probs(n - 2)
                    row_bias(n - 1)
                    outputs_low(n - 2, (j - 2) % STEPS)
                    inverse_sum(n - 1)
                    dve.wait_ge(k_done, n + 1)
                    nc.vector.tensor_copy(kT[:], K_PS[:]).then_inc(k_sbuf, 1)
                    if j <= 1:
                        add_outputs(i, j)
                    if j >= 6:
                        add_outputs(i, j - 4)
            last = PAIRS * STEPS
            copy_probs(last - 2)
            row_bias(last - 1)
            outputs_low(last - 2, STEPS - 2)
            inverse_sum(last - 1)
            add_outputs(PAIRS, 0)
            copy_probs(last - 1)
            outputs_low(last - 1, STEPS - 1)
            add_outputs(PAIRS, 1)

            rms_normalise(2, xs, 4)
            dve.wait_ge(gate_split, 1)
            nc.vector.tensor_tensor(gate_w[1][:], gate_raw[:], gate_w[0][:].bitcast(F32), ALU.subtract).then_inc(gate_split, 1)

            def per_tile(ap):
                return ap[:].rearrange("p (t o) -> p t o", o=1).to_broadcast([P, NT, E])

            dve.wait_ge(logit_done, 1)
            logit_ps = bank[0][:, 0:NT * E].rearrange("p (t e) -> p t e", e=E)
            link(nc.vector.tensor_reduce(lmax[:], logit_ps, mybir.AxisListType.X, ALU.max))
            nc.vector.tensor_tensor(logit[:], logit_ps, per_tile(lmax), ALU.subtract).then_inc(var_ready, 1)
            dve.wait_ge(std_ready, 5)
            link(nc.vector.tensor_reduce(lsum[:], logit[:], mybir.AxisListType.X, ALU.add))
            link(nc.vector.reciprocal(lsum[:], lsum[:]))
            link(nc.vector.tensor_tensor(logit[:], logit[:], per_tile(lsum), ALU.mult))
            for t in range(NT):
                ins = nc.vector.max(best[:, t, :], logit[:, t, :])
            link(ins)
            link(nc.vector.memset(best[:, :, TOPK:8], -1.0))
            for t in range(NT):
                ins = nc.vector.match_replace(rest[:, t, :], best[:, t, :], logit[:, t, :], 0.0)
            link(ins)
            link(nc.vector.tensor_tensor(cw[:], logit[:], rest[:], ALU.subtract))
            link(nc.vector.tensor_reduce(lsum[:], cw[:], mybir.AxisListType.X, ALU.add))
            link(nc.vector.reciprocal(lsum[:], lsum[:]))
            link(nc.vector.tensor_tensor(cw[:], cw[:], per_tile(lsum), ALU.mult))
            link(nc.vector.tensor_copy(cw_hi[:], cw[:]))
            dve.wait_ge(zeroed, 7)
            nc.vector.tensor_copy(cw_rows[:, :, 0:E], cw_hi[:].bitcast(F32))
            nc.vector.memset(cw_rows[:, :, E:E + 1], 1.0)
            nc.vector.tensor_tensor(cw_rows[:, :, SELP // 2:SELP // 2 + E], cw[:], cw_hi[:].bitcast(F32),
                                    ALU.subtract).then_inc(cw_ready, 1)

            def add_group(count, g):
                dve.wait_ge(d_done, count)
                for half in range(2):
                    t = TG * g + 2 * half
                    ins = nc.vector.tensor_tensor(xs[:, t:t + 2, :], pair_of(ACC_PS[half]), xs[:, t:t + 2, :], ALU.add)
                ins.then_inc(acc_added, 1)

            dve.wait_ge(cwT_ready, G)
            dve.wait_ge(zeroed, 11)
            dve.wait_ge(x_copied, NT)
            nc.vector.memset(pause[:, 1:2], 0.0).then_inc(silu_ready, 2)
            nc.vector.memset(pause[:, 2:3], 0.0).then_inc(gated_ready, 2)
            nc.vector.memset(pause[:, 3:4], 0.0).then_inc(hid_ready, 2)
            nc.vector.memset(pause[:, 4:5], 0.0).then_inc(hh_hi, 1)
            nc.vector.memset(pause[:, 5:6], 0.0).then_inc(hh_lo, 1)
            with dve.Fori(0, BODIES) as i:
                for s in range(MSTEPS):
                    g, j, par = s // JB, s % JB, s % 2
                    n = i * MSTEPS + s
                    dve.wait_ge(silu_ready, n + 3)
                    dve.wait_ge(u_done, n + 1)
                    nc.vector.tensor_tensor(gated[:, par, :], U_PS[par][:], silu[:, par, :], ALU.mult).then_inc(gated_ready, 1)
                    dve.wait_ge(gated_ready, n + 3)
                    dve.wait_ge(c_done, n + 1)
                    nc.vector.tensor_tensor(hid[:, par, :], CW_PS[par][:], gated[:, par, :], ALU.mult).then_inc(hid_ready, 1)
                    if j == 0:
                        add_group(n + 1, (g - 1) % G)
                    dve.wait_ge(hh_hi, n + 2)
                    nc.vector.tensor_tensor(hh[1][:, par, :], hid[:, par, :], hh[0][:, par, :].bitcast(F32),
                                            ALU.subtract).then_inc(hh_lo, 1)
            add_group(BODIES * MSTEPS + 1, G - 1)
            dve.wait_ge(acc_added, G * BODIES + 1)
            layernorm(6, xn, final_ready)


def _program(nc, args, out):
    decoder_layer(nc, *args, out)


def kernel(**inputs):
    import numpy as np
    import concourse.bacc as bacc
    from concourse.bass_utils import run_bass_kernel_spmd as run

    a = {k: np.asarray(v) for k, v in inputs.items()}
    f32 = np.float32
    tokens = B * S
    xT = a["x"].reshape(tokens, D).T
    ctxT = a["ctx_2048"].reshape(tokens, D).T
    bands = np.eye(D, dtype=f32).reshape(KD, P, D).transpose(1, 0, 2)
    ident = np.eye(P, dtype=f32)
    mask = np.where(np.arange(S)[None, :] <= np.arange(S)[:, None], 0.0, -1e9 * float(HD) ** 0.5).astype(f32)
    def chunks(w, lo, n):
        return w[:, lo:lo + n].reshape(KD, P, n).transpose(1, 0, 2).reshape(P, KD * n)
    att = np.zeros((PAIRS + 1, P, 2048), f32)
    for p in range(PAIRS):
        parts = []
        for h in (2 * p, 2 * p + 1):
            parts += [chunks(a["L0_ffn_wq"], HD * h, HD), chunks(a["L0_ffn_wk"], HD * h, HD)]
        parts.append(chunks(a["L0_ffn_wv"], 2 * HD * p, 2 * HD))
        parts.append(a["L0_ffn_wo"][2 * HD * p:2 * HD * (p + 1)].reshape(2, HD, D).transpose(1, 0, 2).reshape(P, 2 * D))
        att[p] = np.concatenate(parts, axis=1)
    pad = CT * P - E * I - SI
    def flat(routed, shared):
        return np.concatenate([routed, shared, np.zeros((pad, D), f32)], axis=0)
    wg = flat(a["L0_ffn_eg_w"].reshape(E * I, D), a["L0_ffn_sg_w"])
    wu = flat(a["L0_ffn_eu_w"].reshape(E * I, D), a["L0_ffn_su_w"])
    wd = flat(a["L0_ffn_ed_w"].transpose(0, 2, 1).reshape(E * I, D), a["L0_ffn_sd_w"].T)
    expert = np.minimum(np.arange(CT * P) // I, E)
    sel = np.zeros((P, CT * P), f32)
    sel[expert, np.arange(CT * P)] = 1.0
    low = expert < E
    sel[SELP // 2 + expert[low], np.arange(CT * P)[low]] = 1.0
    moe = np.concatenate([chunks(wg.T, 0, CT * P).reshape(P, KD, CT, P).transpose(0, 2, 1, 3).reshape(P, CT, KD * P),
                          chunks(wu.T, 0, CT * P).reshape(P, KD, CT, P).transpose(0, 2, 1, 3).reshape(P, CT, KD * P),
                          wd.reshape(CT, P, D).transpose(1, 0, 2),
                          sel.reshape(P, CT, P)], axis=2)
    moe_p = np.zeros((BODIES + 1, P, JB, WT), f32)
    moe_p[:BODIES] = moe.reshape(P, BODIES, JB, WT).transpose(1, 0, 2, 3)
    columns = np.stack([a["L0_attn_weight"][0], np.repeat(a["L0_xattn_decay"].reshape(-1), D // a["L0_xattn_decay"].size),
                        a["L0_ffn_ln1_w"], a["L0_ffn_ln2_w"]]).reshape(4, KD, P).transpose(2, 0, 1)
    arrays = {
        "x": a["x"], "xT": xT, "ctxT": ctxT, "bands": bands, "ident": ident, "mask": mask,
        "aw": a["L0_attn_weight"], "bias": a["L0_attn_bias"], "decay": a["L0_attn_decay_value"].reshape(2),
        "columns": columns, "w_att": att,
        "gateT": a["L0_ffn_gate_w"].T.reshape(KD, P, E).transpose(1, 0, 2), "w_moe": moe_p,
    }
    arrays = {k: np.ascontiguousarray(v) for k, v in arrays.items()}
    nc = bacc.Bacc("TRN2", target_bir_lowering=False, num_devices=1)
    args = [nc.dram_tensor(f"in_{k}", v.shape, mybir.dt.from_np(v.dtype), kind="ExternalInput").ap()
            for k, v in arrays.items()]
    out = nc.dram_tensor("out_x", (B, S, D), F32, kind="ExternalOutput").ap()
    _program(nc, args, out)
    r = run(nc, [{f"in_{k}": v for k, v in arrays.items()}], core_ids=[0])
    return r.results[0]["out_x"]
```

```python
from contextlib import ExitStack

import concourse.bass as bass
from concourse import mybir

F32 = mybir.dt.float32
F32R = mybir.dt.float32r
ALU = mybir.AluOpType
ACT = mybir.ActivationFunctionType

P = 128
B, S, D = 16, 128, 256
NT = B * S // P
G = 4
TG = NT // G
N = TG * P
KD = D // P
H, HD = 16, 128
PAIRS = H // 2
STEPS = 2 * G
E, TOPK, I, SI = 16, 6, 176, 352
CT = -(-(E * I + SI) // P)
JB = 5
JB_EARLY = 3
BODIES = CT // JB
MSTEPS = G * JB
WT = 2 * KD * P + D + P
WSPLIT = WT - P
SELP = 64
LN_EPS = 1e-5
RMS_EPS = 1e-6
SCALE = 1.0 / float(HD) ** 0.5
LOWEST = -3.0e38
ROOT_SCALE = 2.0 ** -16
assert NT == B and H % 2 == 0 and CT == JB * BODIES and KD == 2

PRODUCTS = ((0, 0), (0, 1), (1, 0))


def decoder_layer(nc, xT, ctxT, bands, ident_in, mask_in, aw, bias, decay, columns, w_att, gateT, w_moe, out):
    with ExitStack() as ctx:
        def sb(name, shape, dt=F32, at=ctx):
            return at.enter_context(nc.sbuf_tensor(name, shape, dt))

        def sem(name):
            return ctx.enter_context(nc.semaphore(name))

        bank = [ctx.enter_context(nc.psum_tensor(f"bank{n}", [P, N], F32)) for n in range(8)]

        xs = sb("xs", [P, NT, D])
        x2 = sb("x2", [P, NT, D])
        xn = sb("xn", [P, NT, D])
        hT = [sb("hT_hi", [P, KD, NT * P], F32R), sb("hT_lo", [P, KD, NT * P], F32R)]
        ident = sb("ident", [P, P])
        mask = sb("mask", [P, P])
        vec = sb("vec", [P, 4, KD])
        w0_col, xdec, lnw = vec[:, 0, :], vec[:, 1, :], vec[:, 2:4, :]
        stats = sb("stats", [P, NT, 6])
        mv = sb("mv", [P, NT, 2])
        var = sb("var", [P, G, 2 * TG])
        std = sb("std", [P, G, 2 * TG])
        rstd = sb("rstd", [P, G, 2 * TG])
        shift = sb("shift", [P, G, 2 * TG])
        pause = sb("pause", [P, 1])
        gate_raw = sb("gate_raw", [P, KD, E])
        gate_w = [sb("gate_hi", [P, KD, E], F32R), sb("gate_lo", [P, KD, E], F32R)]
        raw_qk = sb("raw_qk", [P, 2, 2, KD, HD])
        raw_v = sb("raw_v", [P, KD, 2 * HD])
        raw_o = sb("raw_o", [P, 2, D])
        w_qk = [sb("w_qk_hi", [P, 2, 2, KD, HD], F32R), sb("w_qk_lo", [P, 2, 2, KD, HD], F32R)]
        w_v = [sb("w_v_hi", [P, KD, 2 * HD], F32R), sb("w_v_lo", [P, KD, 2 * HD], F32R)]
        w_o = [sb("w_o_hi", [P, 2, D], F32R), sb("w_o_lo", [P, 2, D], F32R)]
        raw_m = sb("raw_m", [P, JB, WT])

        with ExitStack() as first:
            xT_sb = sb("xT_sb", [P, KD, NT * P], at=first)
            ctx_sb = sb("ctx_sb", [P, KD, NT * P], at=first)
            run_sb = sb("run_sb", [P, KD, NT * P], at=first)
            band = sb("band", [P, KD, D], at=first)
            pow0 = sb("pow0", [P, KD, D], at=first)
            pow1 = sb("pow1", [P, KD, D], at=first)
            wsum = sb("wsum", [P, KD, D], at=first)
            w1_row = sb("w1_row", [P, D], at=first)
            bias_row = sb("bias_row", [1, D], at=first)
            ones = sb("ones", [1, P], at=first)
            dv = sb("dv", [P, 2], at=first)
        with ExitStack() as second:
            v_sb = sb("v_sb", [P, NT, 2 * HD], at=second)
            qT = sb("qT", [P, N], at=second)
            kT = sb("kT", [P, N], at=second)
            pT = sb("pT", [P, N], at=second)
            oT = [sb("oT_hi", [P, G + 1, N], F32R, second), sb("oT_lo", [P, G + 1, N], F32R, second)]
            prob = sb("prob", [P, TG, S], at=second)
            rowmax = sb("rowmax", [P, TG], at=second)
            nbias = sb("nbias", [P, TG], at=second)
            rowsum = sb("rowsum", [P, TG], at=second)
            rinv = sb("rinv", [P, TG], at=second)
            early = second.enter_context(ExitStack())
            wm = [[sb(f"wm_{part}{j}", [P, w], F32R, early) for j in range(JB_EARLY)] for part, w in (("hi", WT), ("lo", WSPLIT))]
            logit = sb("logit", [P, NT, E], at=early)
            lmax = sb("lmax", [P, NT], at=early)
            lsum = sb("lsum", [P, NT], at=early)
            csum = sb("csum", [P, NT], at=early)
            best = sb("best", [P, NT, 8], at=early)
            rest = sb("rest", [P, NT, E], at=early)
            cw = sb("cw", [P, NT, E], at=early)
            cw_hi = sb("cw_hi", [P, NT, E], F32R, early)
            cw_rows = sb("cw_rows", [P, NT, SELP], at=early)
            cwT = sb("cwT", [SELP, NT * P], F32R, early)
        with ExitStack() as third:
            for part, w in enumerate((WT, WSPLIT)):
                wm[part] += [sb(f"wm_{('hi', 'lo')[part]}{j}", [P, w], F32R, third) for j in range(JB_EARLY, JB)]
            silu = sb("silu", [P, 2, N], at=third)
            gated = sb("gated", [P, 2, N], at=third)
            hid = sb("hid", [P, 2, N], at=third)
            hh = [sb("hh_hi", [P, 2, N], F32R, third), sb("hh_lo", [P, 2, N], F32R, third)]

        Q_PS, K_PS, VO_PS, S_PS, PT_PS, O_PS = bank[0], bank[1], bank[2:4], bank[4], bank[5], bank[6]
        PREP_PS = (bank[2:4], bank[0:2], bank[4:6], bank[6:8])
        G_PS, ACC_PS, U_PS, CW_PS, R_PS = bank[0:2], bank[2:4], bank[4:6], bank[6], bank[7]

        def sems(*names):
            return [sem(n) for n in names]

        ld_decay, ld_small, ld_v, ld_o, ld_moe, ld_gate = sems("ld_decay", "ld_small", "ld_v", "ld_o", "ld_moe", "ld_gate")
        ld_xT, ld_ctx = (sems(*(f"{n}{g}" for g in range(G))) for n in ("ld_xT", "ld_ctx"))
        ld_qk = sems("ld_qk0", "ld_qk1")
        stored = sem("stored")
        dve_chain, ones_ready, ctx_sq, w_ready, xw_done, run_ready, run_T, x_scanned = sems(
            "dve_chain", "ones_ready", "ctx_sq", "w_ready", "xw_done", "run_ready", "run_T", "x_scanned")
        var_ready, std_ready, ln1_ready, x1_ready, ln2_ready, x2_ready = sems(
            "var_ready", "std_ready", "ln1_ready", "x1_ready", "ln2_ready", "x2_ready")
        xn_ready, xn_T, h_hi, h_lo = sems("xn_ready", "xn_T", "h_hi", "h_lo")
        q_done, k_done, s_done, pt_done, o_done, v_done, wo_done = sems(
            "q_done", "k_done", "s_done", "pt_done", "o_done", "v_done", "wo_done")
        q_sbuf, k_sbuf, pt_sbuf, v_sbuf, o_hi, o_lo = sems("q_sbuf", "k_sbuf", "pt_sbuf", "v_sbuf", "o_hi", "o_lo")
        masked, nbias_ready, exp_done, rinv_ready, prob_ready, wo_added = sems(
            "masked", "nbias_ready", "exp_done", "rinv_ready", "prob_ready", "wo_added")
        w_hi_ready, v_ready, o_ready = sems("w_hi_ready", "v_ready", "o_ready")
        qk_ready = sems("qk0_ready", "qk1_ready")
        squared, gate_split, zeroed, logit_done, centred, lexp_done, cw_ready, cw_T, cwT_ready, x_outer = sems(
            "squared", "gate_split", "zeroed", "logit_done", "centred", "lexp_done", "cw_ready", "cw_T", "cwT_ready", "x_outer")
        wm_hi_ready, wm_ready, g_done, u_done, c_done, d_done = sems(
            "wm_hi_ready", "wm_ready", "g_done", "u_done", "c_done", "d_done")
        silu_ready, gated_ready, hid_ready, hh_hi, hh_lo, acc_added, final_ready = sems(
            "silu_ready", "gated_ready", "hid_ready", "hh_hi", "hh_lo", "acc_added", "final_ready")

        def group_of(n):
            return slice(n * N, (n + 1) * N)

        def cols(n, w=P):
            return slice(n * w, (n + 1) * w)

        def row_bcast(ap, n):
            return ap.rearrange("(o n) -> o n", o=1).to_broadcast([P, n])

        def qk_parts(head):
            return raw_qk[:, head], [w[:, head] for w in w_qk]

        def v_parts():
            return raw_v[:], [w[:] for w in w_v]

        def o_parts():
            return raw_o[:], [w[:] for w in w_o]

        block = ctx.enter_context(nc.Block())

        LAST = PAIRS * STEPS
        MLAST = BODIES * MSTEPS

        def tiles(g, half=None):
            return slice(TG * g, TG * (g + 1)) if half is None else slice(TG * g + 2 * half, TG * g + 2 * half + 2)

        def pair_of(ps):
            return ps[:].rearrange("p (t n) -> p t n", t=2)

        def var_order(block, g):
            return (g + 1) + max(0, g - 1) if block == 1 else (g + 1) + min(g + 2, G)

        LATE = range(2, G)


        @block.sync
        def _(sp):
            def load_group(dst, src, signal, g):
                sp.dma_start(dst[:, :, group_of(g)], src.rearrange("(c p) t -> p c t", p=P)[:, :, group_of(g)]).then_inc(signal[g], 16)

            sp.dma_start(dv[:], row_bcast(decay, 2)).then_inc(ld_decay, 16)
            sp.dma_start(vec[:], columns).then_inc(ld_decay, 16)
            sp.dma_start(band[:], bands).then_inc(ld_decay, 16)
            sp.dma_start(w1_row[:], row_bcast(aw[1], D)).then_inc(ld_decay, 16)
            load_group(ctx_sb, ctxT, ld_ctx, 0)
            load_group(xT_sb, xT, ld_xT, 0)
            sp.dma_start(bias_row[:], bias.rearrange("(o n) -> o n", o=1)).then_inc(ld_small, 16)
            sp.dma_start(ident[:], ident_in).then_inc(ld_small, 16)
            sp.dma_start(mask[:], mask_in).then_inc(ld_small, 16)
            for g in range(1, G):
                load_group(ctx_sb, ctxT, ld_ctx, g)
                load_group(xT_sb, xT, ld_xT, g)

            def load_qk(pair, head):
                sp.dma_start(raw_qk[:, head], w_att[pair, :, cols(head, 2 * KD * HD)].rearrange(
                    "p (a c n) -> p a c n", a=2, c=KD)).then_inc(ld_qk[head], 16)

            def load_v(pair):
                sp.dma_start(raw_v[:], w_att[pair, :, cols(2, 2 * KD * HD)].rearrange(
                    "p (c n) -> p c n", c=KD)).then_inc(ld_v, 16)

            def load_o(pair):
                sp.dma_start(raw_o[:], w_att[pair, :, cols(3, 2 * D)].rearrange(
                    "p (a n) -> p a n", a=2)).then_inc(ld_o, 16)

            load_qk(0, 0)
            load_v(0)
            load_qk(0, 1)
            load_o(0)
            sp.dma_start(raw_m[:], w_moe[0]).then_inc(ld_moe, 16)
            sp.dma_start(gate_raw[:], gateT).then_inc(ld_gate, 16)
            with sp.Fori(0, PAIRS - 1) as i:
                sp.wait_ge(qk_ready[0], i + 1)
                load_qk(i + 1, 0)
                sp.wait_ge(v_ready, i + 1)
                load_v(i + 1)
                sp.wait_ge(qk_ready[1], i + 1)
                load_qk(i + 1, 1)
                sp.wait_ge(o_ready, i + 1)
                load_o(i + 1)
            with sp.Fori(1, BODIES) as i:
                sp.wait_ge(wm_ready, i * JB)
                sp.dma_start(raw_m[:], w_moe[i]).then_inc(ld_moe, 16)
            for g in range(G):
                sp.wait_ge(final_ready, TG * (g + 1))
                sp.dma_start(out.rearrange("t p d -> p t d")[:, tiles(g), :], xn[:, tiles(g), :]).then_inc(stored, 16)
            sp.wait_ge(stored, 16 * G)

        @block.tensor
        def _(pe):
            def split_matmul(out_ap, pairs, first=True, last=True, **kw):
                n, total = 0, len(pairs) * len(PRODUCTS)
                for stat, mov in pairs:
                    for a, b in PRODUCTS:
                        mm = nc.tensor.matmul(out_ap, stat(a), mov(b), start=first and n == 0,
                                              stop=last and n == total - 1, **kw)
                        n += 1
                return mm

            def attend_decay(g):
                pe.wait_ge(ld_xT[g], 16)
                for t in range(TG * g, TG * (g + 1)):
                    ps = PREP_PS[g][t % TG // 2][:, cols(t % 2, D)]
                    for c in range(KD):
                        nc.tensor.matmul(ps, xT_sb[:, c, cols(t)], wsum[:, c, :], start=c == 0, stop=False)
                    mm = nc.tensor.matmul(ps, ones[:], bias_row[:], start=False, stop=True)
                    if t % 2:
                        mm.then_inc(xw_done, 1)

            def turn_sums(g):
                pe.wait_ge(run_ready, g + 1)
                pe.wait_ge(x1_ready, TG * (g + 1))
                for t in range(TG * g, TG * (g + 1)):
                    for c in range(KD):
                        mm = nc.tensor.transpose(PREP_PS[g][t % TG // 2][:, D * (t % 2) + P * c:D * (t % 2) + P * (c + 1)],
                                                 run_sb[:, c, cols(t)], ident[:])
                    if t % 2:
                        mm.then_inc(run_T, 1)

            def turn_normed(g, c, ps):
                for b in range(TG):
                    mm = nc.tensor.transpose(ps[:, cols(b)], xn[:, TG * g + b, cols(c)], ident[:])
                mm.then_inc(xn_T, 1)

            def turn_input(g):
                pe.wait_ge(xn_ready, TG * (g + 1))
                for c in range(KD):
                    turn_normed(g, c, PREP_PS[g][c])

            pe.wait_ge(w_ready, KD)
            pe.wait_ge(ld_small, 16 * 3)
            pe.wait_ge(ones_ready, 1)
            attend_decay(0)
            attend_decay(1)
            turn_sums(0)
            attend_decay(2)
            attend_decay(3)
            turn_sums(1)
            for g in range(2, G):
                turn_input(g - 2)
                turn_sums(g)
            turn_input(G - 2)

            def project(j, which, ps, chunks=range(KD)):
                head, g = j // G, j % G
                for c in chunks:
                    mm = split_matmul(ps[:], [(lambda a: w_qk[a][:, head, which, c, :],
                                               lambda b: hT[b][:, c, group_of(g)])], first=c == 0, last=c == KD - 1)
                return mm

            def weighted_values(n, j):
                head, g = j // G, j % G
                pe.wait_ge(pt_sbuf, n + 1)
                for b in range(TG):
                    mm = nc.tensor.matmul(O_PS[:, cols(b)], v_sb[:, TG * g + b, cols(head)], pT[:, cols(b)],
                                          start=True, stop=True)
                mm.then_inc(o_done, 1)

            def transpose_probs(n):
                pe.wait_ge(prob_ready, n + 1)
                for b in range(TG):
                    mm = nc.tensor.transpose(PT_PS[:, cols(b)], prob[:, b, :], ident[:])
                mm.then_inc(pt_done, 1)

            def values(i, g, first):
                for half in range(2):
                    if g:
                        pe.wait_ge(v_sbuf, 2 * G * i + 2 * (g - 1) + half + 1)
                    elif not first:
                        pe.wait_ge(wo_added, 2 * G * i - 2 + half + 1)
                    for b in range(2):
                        t = TG * g + 2 * half + b
                        mm = split_matmul(VO_PS[half][:, cols(b, D)],
                                          [(lambda a, c=c: hT[a][:, c, cols(t)], lambda m, c=c: w_v[m][:, c, :])
                                           for c in range(KD)])
                    mm.then_inc(v_done, 1)

            def project_out(pair, g):
                pe.wait_ge(o_lo, STEPS * pair + G + g + 1)
                for half in range(2):
                    if g:
                        pe.wait_ge(wo_added, 2 * G * pair + 2 * (g - 1) + half + 1)
                    else:
                        pe.wait_ge(v_sbuf, 2 * G * pair + 2 * (G - 1) + half + 1)
                    for b in range(2):
                        t = 2 * half + b
                        mm = split_matmul(VO_PS[half][:, cols(b, D)],
                                          [(lambda a, h=h: oT[a][:, G if h else g, cols(t)], lambda w, h=h: w_o[w][:, h, :])
                                           for h in range(2)])
                    mm.then_inc(wo_done, 1)

            def attention_step(i, j, first):
                n = STEPS * i + j
                if j % G == 0:
                    pe.wait_ge(qk_ready[j // G], i + 1)
                if first and j < G:
                    pe.wait_ge(h_lo, KD * max(j + 1, 2))
                if not first or j >= 1:
                    pe.wait_ge(q_sbuf, n)
                project(j, 0, Q_PS, [0])
                if 2 <= j < G + 2:
                    pe.wait_ge(v_sbuf, 2 * G * i + 2 * (j - 2) + 2)
                if first and j == 2:
                    pe.wait_ge(h_lo, KD * G)
                if not first or j >= 2:
                    weighted_values(n - 2, (j - 2) % STEPS)
                project(j, 0, Q_PS, [1]).then_inc(q_done, 1)
                if not first or j >= 1:
                    pe.wait_ge(k_sbuf, n)
                project(j, 1, K_PS).then_inc(k_done, 1)
                if j < 2 and not first:
                    project_out(i - 1, j + 2)
                if 1 <= j <= G:
                    if j == 1:
                        pe.wait_ge(v_ready, i + 1)
                    values(i, j - 1, first)
                if j >= 6:
                    if j == 6:
                        pe.wait_ge(o_ready, i + 1)
                    project_out(i, j - 6)
                if not first or j >= 1:
                    transpose_probs(n - 1)
                if first and j == 0:
                    pe.wait_ge(h_lo, KD * (G - 1))
                pe.wait_ge(q_sbuf, n + 1)
                pe.wait_ge(k_sbuf, n + 1)
                for b in range(TG):
                    mm = nc.tensor.matmul(S_PS[:, cols(b)], qT[:, cols(b)], kT[:, cols(b)], start=True, stop=True)
                mm.then_inc(s_done, 1)

            for j in range(STEPS):
                attention_step(0, j, True)
                if j == 0:
                    turn_input(G - 1)
            with pe.Fori(1, PAIRS - 1) as i:
                for j in range(STEPS):
                    attention_step(i, j, False)

            def turn_stream(g, c, ps, free=None):
                pe.wait_ge(xn_ready, NT + TG * (g + 1))
                if free is not None:
                    pe.wait_ge(*free)
                turn_normed(g, c, ps)

            def logits(g):
                pe.wait_ge(h_lo, KD * (G + g + 1))
                if g == 0:
                    pe.wait_ge(gate_split, 2)
                for b in range(TG):
                    t = TG * g + b
                    mm = split_matmul(R_PS[:, cols(b, E)], [(lambda a, c=c: hT[a][:, c, cols(t)],
                                                           lambda m, c=c: gate_w[m][:, c, :]) for c in range(KD)])
                mm.then_inc(logit_done, 1)

            def turn_weights(g):
                pe.wait_ge(cw_ready, g + 1)
                for b in range(TG):
                    mm = nc.tensor.transpose(R_PS[0:SELP, cols(b)], cw_rows[:, TG * g + b, :], ident[:])
                mm.then_inc(cw_T, 1)

            def down(n, j, par):
                pe.wait_ge(hh_lo, n + 1)
                for half in range(2):
                    for b in range(2):
                        t = 2 * half + b
                        mm = split_matmul(ACC_PS[half][:, cols(b, D)],
                                          [(lambda a: hh[a][:, par, cols(t)],
                                            lambda m: wm[m][j][:, 2 * KD * P:2 * KD * P + D])],
                                          first=j == 0 and b == 0, last=j == JB - 1, skip_group_check=True)
                mm.then_inc(d_done, 1)

            def gate(i, s, first):
                g, j, par = s // JB, s % JB, s % 2
                if g == 0:
                    pe.wait_ge(wm_ready, JB * i + j + 1)
                if not first or s >= 2:
                    pe.wait_ge(silu_ready, MSTEPS * i + s - 1)
                split_matmul(G_PS[par][:], [(lambda a, c=c: wm[a][j][:, cols(c)],
                                             lambda m, c=c: hT[m][:, c, group_of(g)]) for c in range(KD)]).then_inc(g_done, 1)

            def up(i, s, first):
                g, j, par = s // JB, s % JB, s % 2
                if not first or s >= 2:
                    pe.wait_ge(gated_ready, MSTEPS * i + s - 1)
                split_matmul(U_PS[par][:], [(lambda a, c=c: wm[a][j][:, cols(KD + c)],
                                             lambda m, c=c: hT[m][:, c, group_of(g)]) for c in range(KD)]).then_inc(u_done, 1)

            def weigh(i, s, first):
                g, j, par = s // JB, s % JB, s % 2
                n = MSTEPS * i + s
                if first and j == 0:
                    pe.wait_ge(cwT_ready, g + 1)
                if not first or s >= 1:
                    pe.wait_ge(hid_ready, n)
                nc.tensor.matmul(CW_PS[:], wm[0][j][0:SELP, WSPLIT:WT], cwT[:, group_of(g)],
                                 start=True, stop=True).then_inc(c_done, 1)
                if not first or s >= 1:
                    if j == 1 and (not first or g >= 1):
                        pe.wait_ge(acc_added, G * i + g)
                    down(n - 1, (j - 1) % JB, 1 - par)

            for j in range(STEPS):
                attention_step(PAIRS - 1, j, False)
            turn_stream(0, 0, R_PS)
            turn_stream(0, 1, Q_PS)
            weighted_values(LAST - 2, STEPS - 2)
            project_out(PAIRS - 1, 2)
            transpose_probs(LAST - 1)
            logits(0)
            weighted_values(LAST - 1, STEPS - 1)
            gate(0, 0, True)
            up(0, 0, True)
            project_out(PAIRS - 1, 3)
            gate(0, 1, True)
            turn_weights(0)
            pe.wait_ge(wo_added, 2 * G * PAIRS)
            for s in range(MSTEPS):
                g, j = s // JB, s % JB
                if 0 < s < MSTEPS - 1:
                    gate(0, s + 1, True)
                if s < MSTEPS - 1:
                    up(0, s + 1, True)
                if j == 0 and g:
                    turn_weights(g)
                if g + 1 < G:
                    if j == 1:
                        turn_stream(g + 1, 0, R_PS, (cwT_ready, g + 1))
                    if j == 2:
                        turn_stream(g + 1, 1, R_PS, (h_lo, KD * (G + g + 1) + 1))
                    if j == 3:
                        logits(g + 1)
                weigh(0, s, True)
            with pe.Fori(1, BODIES - 1) as i:
                for s in range(MSTEPS):
                    gate(i, s, False)
                    up(i, s, False)
                    weigh(i, s, False)
            for s in range(MSTEPS):
                gate(BODIES - 1, s, False)
                up(BODIES - 1, s, False)
                weigh(BODIES - 1, s, False)
            down(MLAST - 1, JB - 1, 1)

        @block.scalar
        def _(act):
            copy, square = ACT.Copy, ACT.Square

            def square_context(g):
                act.wait_ge(ld_ctx[g], 16)
                nc.scalar.activation(ctx_sb[:, :, group_of(g)], ctx_sb[:, :, group_of(g)], square).then_inc(ctx_sq, 1)

            def square_root(times, g, w):
                act.wait_ge(var_ready, times)
                nc.scalar.activation(std[:, g, 0:w], var[:, g, 0:w], ACT.Sqrt, scale=ROOT_SCALE).then_inc(std_ready, 1)

            def affine(dst, src, g, at, ready, count, done):
                act.wait_ge(ready, count)
                for b in range(TG):
                    ins = nc.scalar.activation(dst[:, TG * g + b, :], src(b), ACT.Identity,
                                               bias=shift[:, g, at + b:at + b + 1], scale=rstd[:, g, at + b:at + b + 1])
                    ins.then_inc(done, 1)

            def high(norm, g, c, ps):
                act.wait_ge(xn_T, norm * G * KD + KD * g + c + 1)
                nc.scalar.activation(hT[0][:, c, group_of(g)], ps[:], copy, scale=lnw[:, norm, c:c + 1]).then_inc(h_hi, 1)

            def weights_high(loaded, value, raw, parts):
                act.wait_ge(loaded, value)
                nc.scalar.activation(parts[0], raw, copy).then_inc(w_hi_ready, 1)

            for g in range(G):
                square_context(g)
            for t in range(1, G + 3):
                if 4 <= t:
                    for c in range(KD):
                        high(0, t - 4, c, PREP_PS[t - 4][c])
                if 3 <= t:
                    affine(xn, lambda b: xs[:, TG * (t - 3) + b, :], t - 3, TG, ln2_ready, t - 3 + 1, xn_ready)
                if t < G + 1:
                    square_root(var_order(1, t - 1), t - 1, TG)
                if 2 <= t < G + 2:
                    square_root(var_order(2, t - 2), t - 2, 2 * TG)
                if t < G + 1:
                    affine(xs, lambda b: PREP_PS[t - 1][b // 2][:, cols(b % 2, D)], t - 1, 0, ln1_ready, t, x1_ready)
                if t == 2:
                    weights_high(ld_qk[0], 16, *qk_parts(0))
                    weights_high(ld_v, 16, *v_parts())

            def sum_squares(g):
                act.wait_ge(wo_added, 2 * G * (PAIRS - 1) + 2 * (g + 1))
                for b in range(TG):
                    t = TG * g + b
                    ins = nc.scalar.activation(xn[:, t, :], xs[:, t, :], square, accum_out=mv[:, t, 0:1])
                ins.then_inc(squared, 1)

            def stream_root(g):
                square_root(2 * G + g + 1, g, TG)

            def exponentials(n):
                act.wait_ge(nbias_ready, n + 1)
                for b in range(TG):
                    ins = nc.scalar.activation(prob[:, b, :], prob[:, b, :], ACT.Exp, bias=nbias[:, b:b + 1],
                                               scale=SCALE, accum_out=rowsum[:, b:b + 1])
                ins.then_inc(exp_done, 1)

            def attention_step(i, j, first, last=False):
                n = STEPS * i + j
                if last and j == STEPS - 1:
                    sum_squares(0)
                if not first or j >= 1:
                    exponentials(n - 1)
                act.wait_ge(q_done, n + 1)
                nc.scalar.activation(qT[:], Q_PS[:], copy).then_inc(q_sbuf, 1)
                if j == 0:
                    if not first:
                        act.wait_ge(k_done, n)
                    weights_high(ld_qk[1], 16 * i + 16, *qk_parts(1))
                if j == 2:
                    if not first:
                        act.wait_ge(wo_done, 2 * G * i)
                    weights_high(ld_o, 16 * i + 16, *o_parts())
                if j == 4 and not last:
                    act.wait_ge(k_done, n)
                    weights_high(ld_qk[0], 16 * i + 32, *qk_parts(0))
                if j == 5 and not last:
                    weights_high(ld_v, 16 * i + 32, *v_parts())
                if 1 <= j <= G:
                    for half in range(2):
                        act.wait_ge(v_done, 2 * G * i + 2 * (j - 1) + half + 1)
                        nc.scalar.activation(v_sb[:, tiles(j - 1, half), :], pair_of(VO_PS[half]), copy).then_inc(v_sbuf, 1)

            for j in range(STEPS):
                attention_step(0, j, True)
                if j < G:
                    affine(x2, lambda b: xs[:, TG * j + b, :], j, 0, ln2_ready, j + 1, x2_ready)
                elif j - 2 in LATE:
                    affine(xs, lambda b: xs[:, TG * (j - 2) + b, :], j - 2, 0, ln2_ready, j - 1, x2_ready)
                if j == 0:
                    for c in range(KD):
                        high(0, G - 1, c, PREP_PS[G - 1][c])
            with act.Fori(1, PAIRS - 1) as i:
                for j in range(STEPS):
                    attention_step(i, j, False)

            def exponentials_of_logits(g):
                act.wait_ge(centred, g + 1)
                nc.scalar.activation(logit[:, tiles(g), :], logit[:, tiles(g), :], ACT.Exp).then_inc(lexp_done, 1)

            def weight_rows(g):
                act.wait_ge(cw_T, g + 1)
                nc.scalar.activation(cwT[:, group_of(g)], R_PS[0:SELP, :], copy).then_inc(cwT_ready, 1)

            def expert_weights_high(body, j):
                act.wait_ge(ld_moe, body * 16 + 16)
                nc.scalar.activation(wm[0][j][:], raw_m[:, j, :], copy).then_inc(wm_hi_ready, 1)

            for j in range(STEPS):
                attention_step(PAIRS - 1, j, False, last=True)
                if j == 3:
                    act.wait_ge(ld_gate, 16)
                    nc.scalar.activation(gate_w[0][:], gate_raw[:], copy).then_inc(gate_split, 1)
                if 4 <= j < 4 + JB_EARLY:
                    expert_weights_high(0, j - 4)
            stream_root(0)
            high(1, 0, 0, R_PS)
            high(1, 0, 1, Q_PS)
            exponentials(LAST - 1)
            sum_squares(1)
            exponentials_of_logits(0)
            stream_root(1)
            weight_rows(0)
            act.wait_ge(wo_done, 2 * G * PAIRS)

            def expert_step(i, s, first, last=False):
                g, j, par = s // JB, s % JB, s % 2
                n = MSTEPS * i + s
                act.wait_ge(g_done, n + 1)
                if not first or s >= 2:
                    act.wait_ge(gated_ready, n - 1)
                nc.scalar.activation(silu[:, par, :], G_PS[par][:], ACT.Silu).then_inc(silu_ready, 1)
                if first and g + 1 < G and 1 <= j <= KD:
                    high(1, g + 1, j - 1, R_PS)
                if first and g and j == 0:
                    weight_rows(g)
                act.wait_ge(hid_ready, n + 1)
                nc.scalar.activation(hh[0][:, par, :], hid[:, par, :], copy).then_inc(hh_hi, 1)
                if first and s < JB - JB_EARLY:
                    expert_weights_high(i, JB_EARLY + s)
                if s == 0 and not first:
                    act.wait_ge(d_done, n)
                    expert_weights_high(i, JB - 1)
                if s > MSTEPS - JB and not last:
                    act.wait_ge(d_done, n)
                    expert_weights_high(i + 1, j - 1)

            def root(g):
                square_root(3 * G + g + 1, g, TG)

            for s in range(MSTEPS):
                expert_step(0, s, True)
                g, j = s // JB, s % JB
                if j == 2 and g + 2 < G:
                    sum_squares(g + 2)
                if j == 3 and g + 1 < G:
                    exponentials_of_logits(g + 1)
                    if g + 2 < G:
                        stream_root(g + 2)
            with act.Fori(1, BODIES - 1) as i:
                for s in range(MSTEPS):
                    expert_step(i, s, False)
            for s in range(MSTEPS):
                expert_step(BODIES - 1, s, False, last=True)
                if s >= JB and s % JB == 2:
                    root(s // JB - 1)
            root(G - 1)

        @block.gpsimd
        def _(pool):
            def weights_low(value, raw, parts, ready):
                pool.wait_ge(w_hi_ready, value)
                nc.gpsimd.tensor_tensor(parts[1], raw, parts[0].bitcast(F32), ALU.subtract).then_inc(ready, 1)

            nc.gpsimd.memset(ones[:], 1.0).then_inc(ones_ready, 1)
            weights_low(1, *qk_parts(0), qk_ready[0])
            weights_low(2, *v_parts(), v_ready)

            def normalise(n):
                pool.wait_ge(rinv_ready, n + 1)
                nc.gpsimd.tensor_tensor(prob[:], prob[:], rinv[:].rearrange("p (b o) -> p b o", o=1).to_broadcast([P, TG, S]),
                                        ALU.mult).then_inc(prob_ready, 1)

            def attention_step(i, j, first, last=False):
                n = STEPS * i + j
                if not first or j >= 1:
                    normalise(n - 1)
                if j == 0:
                    weights_low(4 * i + 3, *qk_parts(1), qk_ready[1])
                if j == 2:
                    weights_low(4 * i + 4, *o_parts(), o_ready)
                if j == 4 and not last:
                    weights_low(4 * i + 5, *qk_parts(0), qk_ready[0])
                if j == 5 and not last:
                    weights_low(4 * i + 6, *v_parts(), v_ready)

            for j in range(STEPS):
                attention_step(0, j, True)
            with pool.Fori(1, PAIRS - 1) as i:
                for j in range(STEPS):
                    attention_step(i, j, False)

            def expert_weights_low(body, j):
                pool.wait_ge(wm_hi_ready, body * JB + j + 1)
                nc.gpsimd.tensor_tensor(wm[1][j][:], raw_m[:, j, 0:WSPLIT], wm[0][j][:, 0:WSPLIT].bitcast(F32),
                                        ALU.subtract).then_inc(wm_ready, 1)

            def outer_residual(g):
                pool.wait_ge(xn_ready, NT + TG * (g + 1))
                for half in range(2):
                    nc.gpsimd.tensor_tensor(xs[:, tiles(g, half), :], xs[:, tiles(g, half), :], x2[:, tiles(g, half), :],
                                            ALU.add).then_inc(x_outer, 1)

            nc.gpsimd.memset(cw_rows[:], 0.0).then_inc(zeroed, 1)
            for j in range(STEPS):
                attention_step(PAIRS - 1, j, False, last=True)
                if 4 <= j < 4 + JB_EARLY:
                    expert_weights_low(0, j - 4)
            normalise(LAST - 1)
            for j in range(JB_EARLY, JB):
                expert_weights_low(0, j)
            for g in range(G):
                outer_residual(g)
            with pool.Fori(1, BODIES) as i:
                for j in range(JB):
                    expert_weights_low(i, j)

        @block.vector
        def _(dve):
            chain = [0]

            def link(ins):
                chain[0] += 1
                ins.then_inc(dve_chain, 1)
                dve.wait_ge(dve_chain, chain[0])

            def decay_weights():
                dve.wait_ge(ld_decay, 16 * 4)
                link(nc.vector.tensor_scalar(dv[:], dv[:], 0.9, 1.0, ALU.max, ALU.min))
                for c in range(KD):
                    nc.vector.tensor_tensor_scan(pow0[:, c, :], dv[:, 0:1].to_broadcast([P, D]), band[:, c, :], 0.0, ALU.mult, ALU.add)
                    link(nc.vector.tensor_tensor_scan(pow1[:, c, :], dv[:, 1:2].to_broadcast([P, D]), band[:, c, :], 0.0, ALU.mult, ALU.add))
                    link(nc.vector.tensor_tensor(pow1[:, c, :], pow1[:, c, :], w1_row[:], ALU.mult))
                    link(nc.vector.scalar_tensor_tensor(pow0[:, c, :], pow0[:, c, :], w0_col[:, c:c + 1], pow1[:, c, :],
                                                        ALU.mult, ALU.add))
                    nc.vector.tensor_tensor(wsum[:, c, :], pow0[:, c, :], band[:, c, :], ALU.add).then_inc(w_ready, 1)

            def running_sums(g):
                dve.wait_ge(ctx_sq, g + 1)
                for t in range(TG * g, TG * (g + 1)):
                    for c in range(KD):
                        ins = nc.vector.tensor_tensor_scan(run_sb[:, c, cols(t)], xdec[:, c:c + 1].to_broadcast([P, S]),
                                                           ctx_sb[:, c, cols(t)], 0.0, ALU.mult, ALU.add)
                ins.then_inc(run_ready, 1)

            def moments(g, src=lambda t: xs[:, t, :]):
                for t in range(TG * g, TG * (g + 1)):
                    ins = nc.vector.bn_stats(stats[:, t, :], src(t))
                link(ins)
                for t in range(TG * g, TG * (g + 1)):
                    ins = nc.vector.bn_aggr(mv[:, t, :], stats[:, t, :])
                link(ins)

            def invert(g, w, times, refine=True):
                v, r = var[:, g, 0:w], rstd[:, g, 0:w]
                dve.wait_ge(std_ready, times)
                link(nc.vector.reciprocal(r, std[:, g, 0:w]))
                if refine:
                    link(nc.vector.tensor_tensor(v, v, r, ALU.mult))
                    link(nc.vector.tensor_tensor(v, v, r, ALU.mult))
                    link(nc.vector.tensor_scalar(v, v, -0.5 * ROOT_SCALE ** 1.5, 1.5 * ROOT_SCALE ** 0.5, ALU.mult, ALU.add))
                    link(nc.vector.tensor_tensor(r, r, v, ALU.mult))
                else:
                    link(nc.vector.tensor_scalar(r, r, ROOT_SCALE ** 0.5, None, ALU.mult))

            def shifts(g, at, done):
                nc.vector.scalar_tensor_tensor(shift[:, g, at:at + TG], mv[:, tiles(g), 0], -1.0,
                                               rstd[:, g, at:at + TG], ALU.mult, ALU.mult).then_inc(done, 1)

            def first_sum(g):
                dve.wait_ge(xw_done, 2 * g + 2)
                moments(g, lambda t: PREP_PS[g][t % TG // 2][:, cols(t % 2, D)])
                nc.vector.tensor_scalar(var[:, g, 0:TG], mv[:, tiles(g), 1], LN_EPS, None, ALU.add).then_inc(var_ready, 1)

            def first_scale(g):
                invert(g, TG, var_order(1, g), refine=False)
                shifts(g, 0, ln1_ready)

            def second_sum(g):
                dve.wait_ge(x1_ready, TG * (g + 1))
                for half in range(2):
                    dve.wait_ge(run_T, 2 * g + half + 1)
                    nc.vector.scalar_tensor_tensor(xs[:, tiles(g, half), :], pair_of(PREP_PS[g][half]), 1.0,
                                                   xs[:, tiles(g, half), :], ALU.add, ALU.mult).then_inc(x_scanned, 1)
                dve.wait_ge(x_scanned, 2 * g + 2)
                moments(g)
                nc.vector.tensor_scalar(var[:, g, TG:2 * TG], mv[:, tiles(g), 1], 1.0 + RMS_EPS, LN_EPS * RMS_EPS,
                                        ALU.mult, ALU.add)
                nc.vector.tensor_scalar(var[:, g, 0:TG], mv[:, tiles(g), 1], LN_EPS, None, ALU.add).then_inc(var_ready, 1)

            def second_scale(g):
                invert(g, 2 * TG, var_order(2, g))
                nc.vector.scalar_tensor_tensor(shift[:, g, 0:TG], mv[:, tiles(g), 0], -1.0, rstd[:, g, 0:TG], ALU.mult, ALU.mult)
                shifts(g, TG, ln2_ready)

            def low(norm, g, c, ps):
                dve.wait_ge(h_hi, norm * G * KD + KD * g + c + 1)
                nc.vector.scalar_tensor_tensor(hT[1][:, c, group_of(g)], ps[:], lnw[:, norm, c:c + 1],
                                               hT[0][:, c, group_of(g)].bitcast(F32), ALU.mult, ALU.subtract).then_inc(h_lo, 1)

            decay_weights()
            for g in range(G - 1):
                running_sums(g)
            for t in range(G + 3):
                if 3 <= t:
                    second_scale(t - 3)
                if 4 <= t:
                    for c in range(KD):
                        low(0, t - 4, c, PREP_PS[t - 4][c])
                if 2 <= t < G + 2:
                    second_sum(t - 2)
                if 1 <= t < G + 1:
                    first_scale(t - 1)
                if t < G:
                    first_sum(t)
                if t == 0:
                    running_sums(G - 1)

            def stream_variance(g):
                dve.wait_ge(squared, g + 1)
                nc.vector.tensor_scalar(var[:, g, 0:TG], mv[:, tiles(g), 0], 1.0 / D, RMS_EPS, ALU.mult, ALU.add).then_inc(var_ready, 1)

            def stream_scale(g):
                invert(g, TG, 2 * G + g + 1)
                for b in range(TG):
                    t = TG * g + b
                    nc.vector.tensor_scalar(xn[:, t, :], xs[:, t, :], rstd[:, g, b:b + 1], None, ALU.mult).then_inc(xn_ready, 1)

            def copy_probs(n):
                dve.wait_ge(pt_done, n + 1)
                nc.vector.tensor_copy(pT[:], PT_PS[:]).then_inc(pt_sbuf, 1)

            def row_bias(n):
                dve.wait_ge(s_done, n + 1)
                nc.vector.memset(pause[:], 0.0)
                for b in range(TG):
                    ins = nc.vector.tensor_tensor_reduce(prob[:, b, :], S_PS[:, cols(b)], mask[:], 1.0, LOWEST,
                                                         ALU.add, ALU.max, accum_out=rowmax[:, b:b + 1])
                ins.then_inc(masked, 1)
                dve.wait_ge(masked, n + 1)
                nc.vector.tensor_scalar(nbias[:], rowmax[:], -SCALE, None, ALU.mult).then_inc(nbias_ready, 1)

            def split_outputs(n, j):
                slot = j if j < G else G
                dve.wait_ge(o_done, n + 1)
                nc.vector.tensor_copy(oT[0][:, slot, :], O_PS[:]).then_inc(o_hi, 1)
                dve.wait_ge(o_hi, n + 1)
                nc.vector.tensor_tensor(oT[1][:, slot, :], O_PS[:], oT[0][:, slot, :].bitcast(F32),
                                        ALU.subtract).then_inc(o_lo, 1)

            def inverse_sum(n):
                dve.wait_ge(exp_done, n + 1)
                nc.vector.reciprocal(rinv[:], rowsum[:]).then_inc(rinv_ready, 1)

            def add_outputs(pair, g, first=False):
                for half in range(2):
                    if first:
                        dve.wait_ge(x2_ready, TG * (g + 1))
                    dve.wait_ge(wo_done, 2 * G * pair + 2 * g + half + 1)
                    nc.vector.tensor_tensor(xs[:, tiles(g, half), :], pair_of(VO_PS[half]), (x2 if first else xs)[:, tiles(g, half), :],
                                            ALU.add).then_inc(wo_added, 1)

            def attention_step(i, j, first, last=False):
                n = STEPS * i + j
                if not first or j >= 2:
                    copy_probs(n - 2)
                if not first or j >= 1:
                    row_bias(n - 1)
                if not first or j >= 2:
                    split_outputs(n - 2, (j - 2) % STEPS)
                if not first or j >= 1:
                    inverse_sum(n - 1)
                dve.wait_ge(k_done, n + 1)
                nc.vector.tensor_copy(kT[:], K_PS[:]).then_inc(k_sbuf, 1)
                if last and j == STEPS - 1:
                    stream_variance(0)
                    stream_scale(0)
                if j < 2 and not first:
                    add_outputs(i - 1, j + 2)
                if j >= 6:
                    add_outputs(i, j - 6, first)

            for j in range(STEPS):
                attention_step(0, j, True)
                if j == 0:
                    for c in range(KD):
                        low(0, G - 1, c, PREP_PS[G - 1][c])
            dve.wait_ge(x2_ready, TG * (G + len(LATE)))
            with dve.Fori(1, PAIRS - 1) as i:
                for j in range(STEPS):
                    attention_step(i, j, False)

            def per_tile(ap):
                return ap.rearrange("p (t o) -> p t o", o=1).to_broadcast([P, TG, E])

            def centre(g):
                dve.wait_ge(logit_done, g + 1)
                found = R_PS[:, 0:TG * E].rearrange("p (t e) -> p t e", e=E)
                link(nc.vector.tensor_reduce(lmax[:, tiles(g)], found, mybir.AxisListType.X, ALU.max))
                nc.vector.tensor_tensor(logit[:, tiles(g), :], found, per_tile(lmax[:, tiles(g)]), ALU.subtract).then_inc(centred, 1)

            def route(g):
                ts = tiles(g)
                dve.wait_ge(lexp_done, g + 1)
                link(nc.vector.tensor_reduce(lsum[:, ts], logit[:, ts, :], mybir.AxisListType.X, ALU.add))
                link(nc.vector.reciprocal(lsum[:, ts], lsum[:, ts]))
                link(nc.vector.tensor_tensor(logit[:, ts, :], logit[:, ts, :], per_tile(lsum[:, ts]), ALU.mult))
                for t in range(TG * g, TG * (g + 1)):
                    ins = nc.vector.max(best[:, t, :], logit[:, t, :])
                link(ins)
                link(nc.vector.memset(best[:, ts, TOPK:8], -1.0))
                for t in range(TG * g, TG * (g + 1)):
                    ins = nc.vector.match_replace(rest[:, t, :], best[:, t, :], logit[:, t, :], 0.0)
                link(ins)
                link(nc.vector.tensor_tensor(cw[:, ts, :], logit[:, ts, :], rest[:, ts, :], ALU.subtract))
                link(nc.vector.tensor_reduce(csum[:, ts], cw[:, ts, :], mybir.AxisListType.X, ALU.add))
                link(nc.vector.reciprocal(csum[:, ts], csum[:, ts]))
                link(nc.vector.tensor_tensor(cw[:, ts, :], cw[:, ts, :], per_tile(csum[:, ts]), ALU.mult))
                link(nc.vector.tensor_copy(cw_hi[:, ts, :], cw[:, ts, :]))
                dve.wait_ge(zeroed, 1)
                nc.vector.tensor_copy(cw_rows[:, ts, 0:E], cw_hi[:, ts, :].bitcast(F32))
                nc.vector.memset(cw_rows[:, ts, E:E + 1], 1.0)
                nc.vector.tensor_tensor(cw_rows[:, ts, SELP // 2:SELP // 2 + E], cw[:, ts, :], cw_hi[:, ts, :].bitcast(F32),
                                        ALU.subtract).then_inc(cw_ready, 1)

            for j in range(STEPS):
                attention_step(PAIRS - 1, j, False, last=True)
                if j == 4:
                    dve.wait_ge(gate_split, 1)
                    nc.vector.tensor_tensor(gate_w[1][:], gate_raw[:], gate_w[0][:].bitcast(F32), ALU.subtract).then_inc(gate_split, 1)
            copy_probs(LAST - 2)
            row_bias(LAST - 1)
            split_outputs(LAST - 2, STEPS - 2)
            inverse_sum(LAST - 1)
            low(1, 0, 0, R_PS)
            low(1, 0, 1, Q_PS)
            add_outputs(PAIRS - 1, 2)
            stream_variance(1)
            copy_probs(LAST - 1)
            centre(0)
            split_outputs(LAST - 1, STEPS - 1)
            route(0)
            stream_scale(1)
            add_outputs(PAIRS - 1, 3)

            def add_group(count, g, ready=None):
                if ready is not None:
                    dve.wait_ge(x_outer, ready)
                dve.wait_ge(d_done, count)
                for half in range(2):
                    ins = nc.vector.tensor_tensor(xs[:, tiles(g, half), :], pair_of(ACC_PS[half]), xs[:, tiles(g, half), :], ALU.add)
                ins.then_inc(acc_added, 1)

            def expert_step(i, s, first):
                g, j, par = s // JB, s % JB, s % 2
                n = MSTEPS * i + s
                dve.wait_ge(silu_ready, n + 1)
                dve.wait_ge(u_done, n + 1)
                nc.vector.tensor_tensor(gated[:, par, :], U_PS[par][:], silu[:, par, :], ALU.mult).then_inc(gated_ready, 1)
                if first and g + 1 < G:
                    if 1 <= j <= KD:
                        low(1, g + 1, j - 1, R_PS)
                    if j == 3:
                        if g + 2 < G:
                            stream_variance(g + 2)
                        centre(g + 1)
                dve.wait_ge(gated_ready, n + 1)
                dve.wait_ge(c_done, n + 1)
                nc.vector.tensor_tensor(hid[:, par, :], CW_PS[:], gated[:, par, :], ALU.mult).then_inc(hid_ready, 1)
                if j == 0 and (not first or g >= 1):
                    add_group(n, (g - 1) % G, 2 * g if first else None)
                dve.wait_ge(hh_hi, n + 1)
                nc.vector.tensor_tensor(hh[1][:, par, :], hid[:, par, :], hh[0][:, par, :].bitcast(F32),
                                        ALU.subtract).then_inc(hh_lo, 1)

            def last_moments(g):
                dve.wait_ge(acc_added, G * (BODIES - 1) + g + 1)
                moments(g)
                nc.vector.tensor_scalar(var[:, g, 0:TG], mv[:, tiles(g), 1], LN_EPS, None, ALU.add).then_inc(var_ready, 1)

            def last_layernorm(g):
                invert(g, TG, 3 * G + g + 1)
                for b in range(TG):
                    t = TG * g + b
                    nc.vector.tensor_scalar(xn[:, t, :], xs[:, t, :], mv[:, t, 0:1], rstd[:, g, b:b + 1],
                                            ALU.subtract, ALU.mult).then_inc(final_ready, 1)

            for s in range(MSTEPS):
                expert_step(0, s, True)
                g, j = s // JB, s % JB
                if j == 3 and g + 1 < G:
                    route(g + 1)
                if j == 4 and g + 2 < G:
                    stream_scale(g + 2)
            dve.wait_ge(x_outer, 2 * G)
            with dve.Fori(1, BODIES - 1) as i:
                for s in range(MSTEPS):
                    expert_step(i, s, False)
            for s in range(MSTEPS):
                expert_step(BODIES - 1, s, False)
                if s >= JB and s % JB == 1:
                    last_moments(s // JB - 1)
                if s >= JB and s % JB == 3:
                    last_layernorm(s // JB - 1)
            add_group(MLAST, G - 1)
            last_moments(G - 1)
            last_layernorm(G - 1)


def _program(nc, args, out):
    decoder_layer(nc, *args, out)


def kernel(**inputs):
    import numpy as np
    import concourse.bacc as bacc
    from concourse.bass_utils import run_bass_kernel_spmd as run

    a = {k: np.asarray(v) for k, v in inputs.items()}
    f32 = np.float32
    tokens = B * S
    xT = a["x"].reshape(tokens, D).T
    ctxT = a["ctx_2048"].reshape(tokens, D).T
    bands = np.eye(D, dtype=f32).reshape(KD, P, D).transpose(1, 0, 2)
    ident = np.eye(P, dtype=f32)
    mask = np.where(np.arange(S)[None, :] <= np.arange(S)[:, None], 0.0, -1e9 * float(HD) ** 0.5).astype(f32)
    def chunks(w, lo, n):
        return w[:, lo:lo + n].reshape(KD, P, n).transpose(1, 0, 2).reshape(P, KD * n)
    att = np.zeros((PAIRS + 1, P, 2048), f32)
    for p in range(PAIRS):
        parts = []
        for h in (2 * p, 2 * p + 1):
            parts += [chunks(a["L0_ffn_wq"], HD * h, HD), chunks(a["L0_ffn_wk"], HD * h, HD)]
        parts.append(chunks(a["L0_ffn_wv"], 2 * HD * p, 2 * HD))
        parts.append(a["L0_ffn_wo"][2 * HD * p:2 * HD * (p + 1)].reshape(2, HD, D).transpose(1, 0, 2).reshape(P, 2 * D))
        att[p] = np.concatenate(parts, axis=1)
    pad = CT * P - E * I - SI
    def flat(routed, shared):
        return np.concatenate([routed, shared, np.zeros((pad, D), f32)], axis=0)
    wg = flat(a["L0_ffn_eg_w"].reshape(E * I, D), a["L0_ffn_sg_w"])
    wu = flat(a["L0_ffn_eu_w"].reshape(E * I, D), a["L0_ffn_su_w"])
    wd = flat(a["L0_ffn_ed_w"].transpose(0, 2, 1).reshape(E * I, D), a["L0_ffn_sd_w"].T)
    expert = np.minimum(np.arange(CT * P) // I, E)
    sel = np.zeros((P, CT * P), f32)
    sel[expert, np.arange(CT * P)] = 1.0
    low = expert < E
    sel[SELP // 2 + expert[low], np.arange(CT * P)[low]] = 1.0
    moe = np.concatenate([chunks(wg.T, 0, CT * P).reshape(P, KD, CT, P).transpose(0, 2, 1, 3).reshape(P, CT, KD * P),
                          chunks(wu.T, 0, CT * P).reshape(P, KD, CT, P).transpose(0, 2, 1, 3).reshape(P, CT, KD * P),
                          wd.reshape(CT, P, D).transpose(1, 0, 2),
                          sel.reshape(P, CT, P)], axis=2)
    moe_p = np.zeros((BODIES + 1, P, JB, WT), f32)
    moe_p[:BODIES] = moe.reshape(P, BODIES, JB, WT).transpose(1, 0, 2, 3)
    columns = np.stack([a["L0_attn_weight"][0], np.repeat(a["L0_xattn_decay"].reshape(-1), D // a["L0_xattn_decay"].size),
                        a["L0_ffn_ln1_w"], a["L0_ffn_ln2_w"]]).reshape(4, KD, P).transpose(2, 0, 1)
    arrays = {
        "xT": xT, "ctxT": ctxT, "bands": bands, "ident": ident, "mask": mask,
        "aw": a["L0_attn_weight"], "bias": a["L0_attn_bias"], "decay": a["L0_attn_decay_value"].reshape(2),
        "columns": columns, "w_att": att,
        "gateT": a["L0_ffn_gate_w"].T.reshape(KD, P, E).transpose(1, 0, 2), "w_moe": moe_p,
    }
    arrays = {k: np.ascontiguousarray(v) for k, v in arrays.items()}
    nc = bacc.Bacc("TRN2", target_bir_lowering=False, num_devices=1)
    args = [nc.dram_tensor(f"in_{k}", v.shape, mybir.dt.from_np(v.dtype), kind="ExternalInput").ap()
            for k, v in arrays.items()]
    out = nc.dram_tensor("out_x", (B, S, D), F32, kind="ExternalOutput").ap()
    _program(nc, args, out)
    r = run(nc, [{f"in_{k}": v for k, v in arrays.items()}], core_ids=[0])
    return r.results[0]["out_x"]
```

```python
from contextlib import ExitStack

import concourse.bass as bass
from concourse import mybir

F32 = mybir.dt.float32
F32R = mybir.dt.float32r
ALU = mybir.AluOpType
ACT = mybir.ActivationFunctionType

P = 128
B, S, D = 16, 128, 256
NT = B * S // P
G = 4
TG = NT // G
N = TG * P
KD = D // P
H, HD = 16, 128
PAIRS = H // 2
STEPS = 2 * G
E, TOPK, I, SI = 16, 6, 176, 352
CT = -(-(E * I + SI) // P)
JB = 5
JB_EARLY = 3
BODIES = CT // JB
MSTEPS = G * JB
WT = 2 * KD * P + D + P
WSPLIT = WT - P
SELP = 2 * E
SHARED = CT - E * I // P
LN_EPS = 1e-5
RMS_EPS = 1e-6
SCALE = 1.0 / float(HD) ** 0.5
LOWEST = -3.0e38
ROOT_SCALE = 2.0 ** -16
assert NT == B and H % 2 == 0 and CT == JB * BODIES and KD == 2 and E * I % P == 0 and SHARED <= JB

PRODUCTS = ((0, 0), (0, 1), (1, 0))


def decoder_layer(nc, xT, ctxT, bands, ident_in, mask_in, aw, bias, decay, columns, w_att, gateT, w_moe, out):
    with ExitStack() as ctx:
        def sb(name, shape, dt=F32, at=ctx):
            return at.enter_context(nc.sbuf_tensor(name, shape, dt))

        def sem(name):
            return ctx.enter_context(nc.semaphore(name))

        bank = [ctx.enter_context(nc.psum_tensor(f"bank{n}", [P, N], F32)) for n in range(8)]

        xs = sb("xs", [P, NT, D])
        x2 = sb("x2", [P, NT, D])
        xn = sb("xn", [P, NT, D])
        hT = [sb("hT_hi", [P, KD, NT * P], F32R), sb("hT_lo", [P, KD, NT * P], F32R)]
        ident = sb("ident", [P, P])
        mask = sb("mask", [P, P])
        vec = sb("vec", [P, 4, KD])
        w0_col, xdec, lnw = vec[:, 0, :], vec[:, 1, :], vec[:, 2:4, :]
        stats = sb("stats", [P, NT, 6])
        mv = sb("mv", [P, NT, 2])
        var = sb("var", [P, G, 2 * TG])
        std = sb("std", [P, G, 2 * TG])
        rstd = sb("rstd", [P, G, 2 * TG])
        shift = sb("shift", [P, G, 2 * TG])
        pause = sb("pause", [P, 1])
        gate_raw = sb("gate_raw", [P, KD, E])
        gate_w = [sb("gate_hi", [P, KD, E], F32R), sb("gate_lo", [P, KD, E], F32R)]
        raw_qk = sb("raw_qk", [P, 2, 2, KD, HD])
        raw_v = sb("raw_v", [P, KD, 2 * HD])
        raw_o = sb("raw_o", [P, 2, D])
        w_qk = [sb("w_qk_hi", [P, 2, 2, KD, HD], F32R), sb("w_qk_lo", [P, 2, 2, KD, HD], F32R)]
        w_v = [sb("w_v_hi", [P, KD, 2 * HD], F32R), sb("w_v_lo", [P, KD, 2 * HD], F32R)]
        w_o = [sb("w_o_hi", [P, 2, D], F32R), sb("w_o_lo", [P, 2, D], F32R)]
        raw_m = sb("raw_m", [P, JB, WT])

        with ExitStack() as first:
            xT_sb = sb("xT_sb", [P, KD, NT * P], at=first)
            ctx_sb = sb("ctx_sb", [P, KD, NT * P], at=first)
            run_sb = sb("run_sb", [P, KD, NT * P], at=first)
            band = sb("band", [P, KD, D], at=first)
            pow0 = sb("pow0", [P, KD, D], at=first)
            pow1 = sb("pow1", [P, KD, D], at=first)
            wsum = sb("wsum", [P, KD, D], at=first)
            w1_row = sb("w1_row", [P, D], at=first)
            bias_row = sb("bias_row", [1, D], at=first)
            bias_part = [sb("bias_hi", [1, D], F32R, first), sb("bias_lo", [1, D], F32R, first)]
            ones = sb("ones", [1, P], F32R, first)
            dv = sb("dv", [P, 2], at=first)
        with ExitStack() as second:
            v_sb = sb("v_sb", [P, NT, 2 * HD], at=second)
            qT = sb("qT", [P, N], at=second)
            kT = sb("kT", [P, N], at=second)
            pT = sb("pT", [P, N], at=second)
            oT = [sb("oT_hi", [P, G + 1, N], F32R, second), sb("oT_lo", [P, G + 1, N], F32R, second)]
            prob = sb("prob", [P, TG, S], at=second)
            rowmax = sb("rowmax", [P, TG], at=second)
            nbias = sb("nbias", [P, TG], at=second)
            rowsum = sb("rowsum", [P, TG], at=second)
            rinv = sb("rinv", [P, TG], at=second)
            early = second.enter_context(ExitStack())
            wm = [[sb(f"wm_{part}{j}", [P, w], F32R, early) for j in range(JB_EARLY)] for part, w in (("hi", WT), ("lo", WSPLIT))]
            logitT = sb("logitT", [E, N], at=early)
            logit = sb("logit", [P, NT, E], at=early)
            lmax = sb("lmax", [P, NT], at=early)
            lsum = sb("lsum", [P, NT], at=early)
            csum = sb("csum", [P, NT], at=early)
            best = sb("best", [P, NT, 8], at=early)
            rest = sb("rest", [P, NT, E], at=early)
            cw = sb("cw", [P, NT, E], at=early)
            cw_hi = sb("cw_hi", [P, NT, E], F32R, early)
            cw_rows = sb("cw_rows", [P, NT, SELP], at=early)
            cwT = sb("cwT", [SELP, NT * P], F32R, early)
        with ExitStack() as third:
            for part, w in enumerate((WT, WSPLIT)):
                wm[part] += [sb(f"wm_{('hi', 'lo')[part]}{j}", [P, w], F32R, third) for j in range(JB_EARLY, JB)]
            silu = sb("silu", [P, 2, N], at=third)
            gated = sb("gated", [P, 2, N], at=third)
            hid = sb("hid", [P, 2, N], at=third)
            hh = [sb("hh_hi", [P, 2, N], F32R, third), sb("hh_lo", [P, 2, N], F32R, third)]

        Q_PS, K_PS, VO_PS, S_PS, PT_PS, O_PS = bank[0], bank[1], bank[2:4], bank[4], bank[5], bank[6]
        PREP_PS = (bank[2:4], bank[0:2], bank[4:6], bank[6:8])
        G_PS, ACC_PS, U_PS, CW_PS, R_PS = bank[0:2], bank[2:4], bank[4:6], bank[6], bank[7]

        def sems(*names):
            return [sem(n) for n in names]

        ld_bias, ld_decay, ld_small, ld_v, ld_o, ld_moe, ld_gate = sems(
            "ld_bias", "ld_decay", "ld_small", "ld_v", "ld_o", "ld_moe", "ld_gate")
        ld_xT, ld_ctx = (sems(*(f"{n}{g}" for g in range(G))) for n in ("ld_xT", "ld_ctx"))
        ld_qk = sems("ld_qk0", "ld_qk1")
        stored = sem("stored")
        dve_chain, bias_ready, ctx_sq, w_ready, xw_done, run_ready, run_T, x_scanned = sems(
            "dve_chain", "bias_ready", "ctx_sq", "w_ready", "xw_done", "run_ready", "run_T", "x_scanned")
        var_ready, std_ready, ln1_ready, x1_ready, ln2_ready, x2_ready = sems(
            "var_ready", "std_ready", "ln1_ready", "x1_ready", "ln2_ready", "x2_ready")
        xn_ready, xn_T, h_hi, h_lo = sems("xn_ready", "xn_T", "h_hi", "h_lo")
        q_done, k_done, s_done, pt_done, o_done, v_done, wo_done = sems(
            "q_done", "k_done", "s_done", "pt_done", "o_done", "v_done", "wo_done")
        q_sbuf, k_sbuf, pt_sbuf, v_sbuf, o_hi, o_lo = sems("q_sbuf", "k_sbuf", "pt_sbuf", "v_sbuf", "o_hi", "o_lo")
        masked, nbias_ready, exp_done, rinv_ready, prob_ready, wo_added = sems(
            "masked", "nbias_ready", "exp_done", "rinv_ready", "prob_ready", "wo_added")
        w_hi_ready, v_ready, o_ready = sems("w_hi_ready", "v_ready", "o_ready")
        qk_ready = sems("qk0_ready", "qk1_ready")
        squared, scale_ready, gate_split, logit_done, logit_sbuf, logit_T = sems(
            "squared", "scale_ready", "gate_split", "logit_done", "logit_sbuf", "logit_T")
        centred, lexp_done, cw_ready, cw_T, cwT_ready, x_outer = sems(
            "centred", "lexp_done", "cw_ready", "cw_T", "cwT_ready", "x_outer")
        wm_hi_ready, wm_ready, g_done, u_done, c_done, d_done, d_half = sems(
            "wm_hi_ready", "wm_ready", "g_done", "u_done", "c_done", "d_done", "d_half")
        silu_ready, gated_ready, hid_ready, hh_hi, hh_lo, acc_added, final_ready, last_scaled, applied = sems(
            "silu_ready", "gated_ready", "hid_ready", "hh_hi", "hh_lo", "acc_added", "final_ready", "last_scaled", "applied")

        def group_of(n):
            return slice(n * N, (n + 1) * N)

        def cols(n, w=P):
            return slice(n * w, (n + 1) * w)

        def row_bcast(ap, n):
            return ap.rearrange("(o n) -> o n", o=1).to_broadcast([P, n])

        def qk_parts(head):
            return raw_qk[:, head], [w[:, head] for w in w_qk]

        def v_parts():
            return raw_v[:], [w[:] for w in w_v]

        def o_parts():
            return raw_o[:], [w[:] for w in w_o]

        block = ctx.enter_context(nc.Block())

        LAST = PAIRS * STEPS
        MLAST = BODIES * MSTEPS

        def tiles(g, half=None):
            return slice(TG * g, TG * (g + 1)) if half is None else slice(TG * g + 2 * half, TG * g + 2 * half + 2)

        def pair_of(ps):
            return ps[:].rearrange("p (t n) -> p t n", t=2)

        def var_order(block, g):
            return (g + 1) + max(0, g - 1) if block == 1 else (g + 1) + min(g + 2, G)

        LATE = range(2, G)
        AHEAD = G + 2

        def shared(s, last):
            return last and s % JB >= JB - SHARED

        def weighed(i, s, last):
            return MSTEPS * i + ((s // JB) * (JB - SHARED) + min(s % JB, JB - SHARED) if last else s)


        @block.sync
        def _(sp):
            def load_group(dst, src, signal, g):
                sp.dma_start(dst[:, :, group_of(g)], src.rearrange("(c p) t -> p c t", p=P)[:, :, group_of(g)]).then_inc(signal[g], 16)

            sp.dma_start(bias_row[:], bias.rearrange("(o n) -> o n", o=1)).then_inc(ld_bias, 16)
            sp.dma_start(dv[:], row_bcast(decay, 2)).then_inc(ld_decay, 16)
            sp.dma_start(vec[:], columns).then_inc(ld_decay, 16)
            sp.dma_start(band[:], bands).then_inc(ld_decay, 16)
            sp.dma_start(w1_row[:], row_bcast(aw[1], D)).then_inc(ld_decay, 16)
            load_group(ctx_sb, ctxT, ld_ctx, 0)
            load_group(xT_sb, xT, ld_xT, 0)
            sp.dma_start(ident[:], ident_in).then_inc(ld_small, 16)
            sp.dma_start(mask[:], mask_in).then_inc(ld_small, 16)
            for g in range(1, G):
                load_group(ctx_sb, ctxT, ld_ctx, g)
                load_group(xT_sb, xT, ld_xT, g)

            def load_qk(pair, head):
                sp.dma_start(raw_qk[:, head], w_att[pair, :, cols(head, 2 * KD * HD)].rearrange(
                    "p (a c n) -> p a c n", a=2, c=KD)).then_inc(ld_qk[head], 16)

            def load_v(pair):
                sp.dma_start(raw_v[:], w_att[pair, :, cols(2, 2 * KD * HD)].rearrange(
                    "p (c n) -> p c n", c=KD)).then_inc(ld_v, 16)

            def load_o(pair):
                sp.dma_start(raw_o[:], w_att[pair, :, cols(3, 2 * D)].rearrange(
                    "p (a n) -> p a n", a=2)).then_inc(ld_o, 16)

            load_qk(0, 0)
            load_v(0)
            load_qk(0, 1)
            load_o(0)
            sp.dma_start(raw_m[:], w_moe[0]).then_inc(ld_moe, 16)
            sp.dma_start(gate_raw[:], gateT).then_inc(ld_gate, 16)
            with sp.Fori(0, PAIRS - 1) as i:
                sp.wait_ge(qk_ready[0], i + 1)
                load_qk(i + 1, 0)
                sp.wait_ge(v_ready, i + 1)
                load_v(i + 1)
                sp.wait_ge(qk_ready[1], i + 1)
                load_qk(i + 1, 1)
                sp.wait_ge(o_ready, i + 1)
                load_o(i + 1)
            with sp.Fori(1, BODIES) as i:
                sp.wait_ge(wm_ready, i * JB)
                sp.dma_start(raw_m[:], w_moe[i]).then_inc(ld_moe, 16)
            stores = [(tiles(g), final_ready, TG * (g + 1)) for g in range(G - 2)] + [(tiles(G - 2), applied, TG)] + [
                (tiles(G - 1, half), final_ready, TG * (G - 2) + 2 * (half + 1)) for half in range(2)]
            for ts, through, count in stores:
                sp.wait_ge(through, count)
                sp.dma_start(out.rearrange("t p d -> p t d")[:, ts, :], xn[:, ts, :]).then_inc(stored, 16)
            sp.wait_ge(stored, 16 * len(stores))

        @block.tensor
        def _(pe):
            def split_matmul(out_ap, pairs, first=True, last=True, **kw):
                n, total = 0, len(pairs) * len(PRODUCTS)
                for stat, mov in pairs:
                    for a, b in PRODUCTS:
                        mm = nc.tensor.matmul(out_ap, stat(a), mov(b), start=first and n == 0,
                                              stop=last and n == total - 1, **kw)
                        n += 1
                return mm

            def attend_decay(g):
                pe.wait_ge(ld_xT[g], 16)
                for t in range(TG * g, TG * (g + 1)):
                    ps = PREP_PS[g][t % TG // 2][:, cols(t % 2, D)]
                    for c in range(KD):
                        nc.tensor.matmul(ps, xT_sb[:, c, cols(t)], wsum[:, c, :], start=c == 0, stop=False)
                    for part in range(2):
                        mm = nc.tensor.matmul(ps, ones[:], bias_part[part][:], start=False, stop=part == 1)
                    if t % 2:
                        mm.then_inc(xw_done, 1)

            def turn_sums(g):
                pe.wait_ge(run_ready, g + 1)
                pe.wait_ge(x1_ready, TG * (g + 1))
                for t in range(TG * g, TG * (g + 1)):
                    for c in range(KD):
                        mm = nc.tensor.transpose(PREP_PS[g][t % TG // 2][:, D * (t % 2) + P * c:D * (t % 2) + P * (c + 1)],
                                                 run_sb[:, c, cols(t)], ident[:])
                    if t % 2:
                        mm.then_inc(run_T, 1)

            def turn_normed(g, c, ps):
                for b in range(TG):
                    mm = nc.tensor.transpose(ps[:, cols(b)], xn[:, TG * g + b, cols(c)], ident[:])
                mm.then_inc(xn_T, 1)

            def turn_input(g):
                pe.wait_ge(xn_ready, TG * (g + 1))
                for c in range(KD):
                    turn_normed(g, c, PREP_PS[g][c])

            pe.wait_ge(w_ready, KD)
            pe.wait_ge(ld_small, 16 * 2)
            pe.wait_ge(bias_ready, 3)
            attend_decay(0)
            attend_decay(1)
            turn_sums(0)
            attend_decay(2)
            turn_sums(1)
            attend_decay(3)
            for g in range(2, G):
                turn_input(g - 2)
                turn_sums(g)
            turn_input(G - 2)

            def project(j, which, ps, chunks=range(KD)):
                head, g = j // G, j % G
                for c in chunks:
                    mm = split_matmul(ps[:], [(lambda a: w_qk[a][:, head, which, c, :],
                                               lambda b: hT[b][:, c, group_of(g)])], first=c == 0, last=c == KD - 1)
                return mm

            def weighted_values(n, j):
                head, g = j // G, j % G
                pe.wait_ge(pt_sbuf, n + 1)
                for b in range(TG):
                    mm = nc.tensor.matmul(O_PS[:, cols(b)], v_sb[:, TG * g + b, cols(head)], pT[:, cols(b)],
                                          start=True, stop=True)
                mm.then_inc(o_done, 1)

            def transpose_probs(n):
                pe.wait_ge(prob_ready, n + 1)
                for b in range(TG):
                    mm = nc.tensor.transpose(PT_PS[:, cols(b)], prob[:, b, :], ident[:])
                mm.then_inc(pt_done, 1)

            def values(i, g, first):
                for half in range(2):
                    if g:
                        pe.wait_ge(v_sbuf, 2 * G * i + 2 * (g - 1) + half + 1)
                    elif not first:
                        pe.wait_ge(wo_added, 2 * G * i - 2 + half + 1)
                    for b in range(2):
                        t = TG * g + 2 * half + b
                        mm = split_matmul(VO_PS[half][:, cols(b, D)],
                                          [(lambda a, c=c: hT[a][:, c, cols(t)], lambda m, c=c: w_v[m][:, c, :])
                                           for c in range(KD)])
                    mm.then_inc(v_done, 1)

            def project_out(pair, g):
                for half in range(2):
                    if g:
                        pe.wait_ge(wo_added, 2 * G * pair + 2 * (g - 1) + half + 1)
                    else:
                        pe.wait_ge(v_sbuf, 2 * G * pair + 2 * (G - 1) + half + 1)
                    for h in range(2):
                        if h and half == 0:
                            pe.wait_ge(o_lo, STEPS * pair + G + g + 1)
                        for b in range(2):
                            t = 2 * half + b
                            mm = split_matmul(VO_PS[half][:, cols(b, D)],
                                              [(lambda a: oT[a][:, G if h else g, cols(t)], lambda w: w_o[w][:, h, :])],
                                              first=h == 0 and b == 0, last=h == 1, skip_group_check=True)
                    mm.then_inc(wo_done, 1)

            def attention_step(i, j, first):
                n = STEPS * i + j
                if j % G == 0:
                    pe.wait_ge(qk_ready[j // G], i + 1)
                if first and j < G:
                    pe.wait_ge(h_lo, KD * max(j + 1, 2))
                if j != AHEAD:
                    if not first or j >= 1:
                        pe.wait_ge(q_sbuf, n)
                    project(j, 0, Q_PS, [0])
                if 2 <= j < G + 2:
                    pe.wait_ge(v_sbuf, 2 * G * i + 2 * (j - 2) + 2)
                if first and j == 2:
                    pe.wait_ge(h_lo, KD * G)
                if not first or j >= 2:
                    weighted_values(n - 2, (j - 2) % STEPS)
                if j != AHEAD:
                    project(j, 0, Q_PS, [1]).then_inc(q_done, 1)
                if not first or j >= 1:
                    pe.wait_ge(k_sbuf, n)
                project(j, 1, K_PS).then_inc(k_done, 1)
                if j + 1 == AHEAD:
                    project(AHEAD, 0, R_PS).then_inc(q_done, 1)
                if j < 2 and not first:
                    project_out(i - 1, j + 2)
                if 1 <= j <= G:
                    if j == 1:
                        pe.wait_ge(v_ready, i + 1)
                    values(i, j - 1, first)
                if j >= 6:
                    if j == 6:
                        pe.wait_ge(o_ready, i + 1)
                    project_out(i, j - 6)
                if not first or j >= 1:
                    transpose_probs(n - 1)
                if first and j == 0:
                    pe.wait_ge(h_lo, KD * (G - 1))
                pe.wait_ge(q_sbuf, n + 1)
                pe.wait_ge(k_sbuf, n + 1)
                for b in range(TG):
                    mm = nc.tensor.matmul(S_PS[:, cols(b)], qT[:, cols(b)], kT[:, cols(b)], start=True, stop=True)
                mm.then_inc(s_done, 1)

            for j in range(STEPS):
                attention_step(0, j, True)
                if j == 0:
                    turn_input(G - 1)
            with pe.Fori(1, PAIRS - 1) as i:
                for j in range(STEPS):
                    attention_step(i, j, False)

            def turn_stream(g, c, ps, free=None):
                pe.wait_ge(xn_ready, NT + TG * (g + 1))
                if free is not None:
                    pe.wait_ge(*free)
                turn_normed(g, c, ps)

            def logits(g):
                pe.wait_ge(h_lo, KD * (G + g + 1))
                if g == 0:
                    pe.wait_ge(gate_split, 2)
                split_matmul(R_PS[0:E, :], [(lambda a, c=c: gate_w[a][:, c, :],
                                             lambda m, c=c: hT[m][:, c, group_of(g)]) for c in range(KD)]).then_inc(logit_done, 1)

            def turn_logits(g):
                pe.wait_ge(logit_sbuf, g + 1)
                for b in range(TG):
                    mm = nc.tensor.transpose(R_PS[:, cols(b, E)], logitT[:, cols(b)], ident[0:E, 0:E])
                mm.then_inc(logit_T, 1)

            def turn_weights(g):
                pe.wait_ge(cw_ready, g + 1)
                for b in range(TG):
                    mm = nc.tensor.transpose(R_PS[0:SELP, cols(b)], cw_rows[:, TG * g + b, :], ident[:])
                mm.then_inc(cw_T, 1)

            def down(n, j, par, half_done=None):
                pe.wait_ge(hh_lo, n + 1)
                for half in range(2):
                    for b in range(2):
                        t = 2 * half + b
                        mm = split_matmul(ACC_PS[half][:, cols(b, D)],
                                          [(lambda a: hh[a][:, par, cols(t)],
                                            lambda m: wm[m][j][:, 2 * KD * P:2 * KD * P + D])],
                                          first=j == 0 and b == 0, last=j == JB - 1, skip_group_check=True)
                    if half_done is not None and half == 0:
                        mm.then_inc(half_done, 1)
                mm.then_inc(d_done, 1)

            def gate(i, s, first):
                g, j, par = s // JB, s % JB, s % 2
                if g == 0:
                    pe.wait_ge(wm_ready, JB * i + j + 1)
                if not first or s >= 2:
                    pe.wait_ge(silu_ready, MSTEPS * i + s - 1)
                split_matmul(G_PS[par][:], [(lambda a, c=c: wm[a][j][:, cols(c)],
                                             lambda m, c=c: hT[m][:, c, group_of(g)]) for c in range(KD)]).then_inc(g_done, 1)

            def up(i, s, first):
                g, j, par = s // JB, s % JB, s % 2
                if not first or s >= 2:
                    pe.wait_ge(gated_ready, MSTEPS * i + s - 1)
                split_matmul(U_PS[par][:], [(lambda a, c=c: wm[a][j][:, cols(KD + c)],
                                             lambda m, c=c: hT[m][:, c, group_of(g)]) for c in range(KD)]).then_inc(u_done, 1)

            def weigh(i, s, first, last=False):
                g, j, par = s // JB, s % JB, s % 2
                n = MSTEPS * i + s
                if first and j == 0 and g:
                    down(n - 1, JB - 1, 1 - par)
                if first and j == 0:
                    pe.wait_ge(cwT_ready, g + 1)
                if not shared(s, last):
                    if not first or s >= 1:
                        pe.wait_ge(hid_ready, weighed(i, s, last))
                    nc.tensor.matmul(CW_PS[:], wm[0][j][0:SELP, WSPLIT:WT], cwT[:, group_of(g)],
                                     start=True, stop=True).then_inc(c_done, 1)
                if not first or j >= 1:
                    if j == 1 and (not first or g >= 1):
                        pe.wait_ge(acc_added, G * i + g)
                    down(n - 1, (j - 1) % JB, 1 - par)

            for j in range(STEPS):
                attention_step(PAIRS - 1, j, False)
            weighted_values(LAST - 2, STEPS - 2)
            turn_stream(0, 0, R_PS)
            turn_stream(0, 1, Q_PS)
            project_out(PAIRS - 1, 2)
            transpose_probs(LAST - 1)
            logits(0)
            weighted_values(LAST - 1, STEPS - 1)
            turn_logits(0)
            gate(0, 0, True)
            up(0, 0, True)
            project_out(PAIRS - 1, 3)
            gate(0, 1, True)
            turn_weights(0)
            for s in range(MSTEPS):
                g, j = s // JB, s % JB
                if 0 < s < MSTEPS - 1:
                    gate(0, s + 1, True)
                if s < MSTEPS - 1:
                    up(0, s + 1, True)
                if j == 0 and g:
                    turn_weights(g)
                if g + 1 < G:
                    if j == 1:
                        turn_stream(g + 1, 0, R_PS, (cwT_ready, g + 1))
                    if j == 2:
                        turn_stream(g + 1, 1, R_PS, (h_lo, KD * (G + g + 1) + 1))
                    if j == 3:
                        logits(g + 1)
                if s == 1:
                    pe.wait_ge(wo_added, 2 * G * PAIRS)
                weigh(0, s, True)
                if j == 3 and g + 1 < G:
                    turn_logits(g + 1)
            with pe.Fori(1, BODIES - 1) as i:
                for s in range(MSTEPS):
                    gate(i, s, False)
                    up(i, s, False)
                    weigh(i, s, False)
            gate(BODIES - 1, 0, False)
            up(BODIES - 1, 0, False)
            for s in range(MSTEPS):
                if s < MSTEPS - 1:
                    gate(BODIES - 1, s + 1, False)
                    up(BODIES - 1, s + 1, False)
                weigh(BODIES - 1, s, False, last=True)
            down(MLAST - 1, JB - 1, 1, half_done=d_half)

        @block.scalar
        def _(act):
            copy, square = ACT.Copy, ACT.Square

            def square_context(g):
                act.wait_ge(ld_ctx[g], 16)
                nc.scalar.activation(ctx_sb[:, :, group_of(g)], ctx_sb[:, :, group_of(g)], square).then_inc(ctx_sq, 1)

            def square_root(times, g, w):
                act.wait_ge(var_ready, times)
                nc.scalar.activation(std[:, g, 0:w], var[:, g, 0:w], ACT.Sqrt, scale=ROOT_SCALE).then_inc(std_ready, 1)

            def affine(dst, src, g, at, ready, count, done):
                act.wait_ge(ready, count)
                for b in range(TG):
                    ins = nc.scalar.activation(dst[:, TG * g + b, :], src(b), ACT.Identity,
                                               bias=shift[:, g, at + b:at + b + 1], scale=rstd[:, g, at + b:at + b + 1])
                    ins.then_inc(done, 1)

            def high(norm, g, c, ps):
                act.wait_ge(xn_T, norm * G * KD + KD * g + c + 1)
                nc.scalar.activation(hT[0][:, c, group_of(g)], ps[:], copy, scale=lnw[:, norm, c:c + 1]).then_inc(h_hi, 1)

            def weights_high(loaded, value, raw, parts):
                act.wait_ge(loaded, value)
                nc.scalar.activation(parts[0], raw, copy).then_inc(w_hi_ready, 1)

            for g in range(G):
                square_context(g)
            for t in range(1, G + 3):
                if 4 <= t:
                    for c in range(KD):
                        high(0, t - 4, c, PREP_PS[t - 4][c])
                if 3 <= t:
                    affine(xn, lambda b: xs[:, TG * (t - 3) + b, :], t - 3, TG, ln2_ready, t - 3 + 1, xn_ready)
                if t < G + 1:
                    square_root(var_order(1, t - 1), t - 1, TG)
                if 2 <= t < G + 2:
                    square_root(var_order(2, t - 2), t - 2, 2 * TG)
                if t < G + 1:
                    affine(xs, lambda b: PREP_PS[t - 1][b // 2][:, cols(b % 2, D)], t - 1, 0, ln1_ready, t, x1_ready)
                if t == 2:
                    weights_high(ld_qk[0], 16, *qk_parts(0))
                    weights_high(ld_v, 16, *v_parts())

            def sum_squares(g):
                act.wait_ge(wo_added, 2 * G * (PAIRS - 1) + 2 * (g + 1))
                for b in range(TG):
                    t = TG * g + b
                    ins = nc.scalar.activation(xn[:, t, :], xs[:, t, :], square, accum_out=mv[:, t, 0:1])
                ins.then_inc(squared, 1)

            def stream_root(g):
                square_root(2 * G + g + 1, g, TG)

            def exponentials(n):
                act.wait_ge(nbias_ready, n + 1)
                for b in range(TG):
                    ins = nc.scalar.activation(prob[:, b, :], prob[:, b, :], ACT.Exp, bias=nbias[:, b:b + 1],
                                               scale=SCALE, accum_out=rowsum[:, b:b + 1])
                ins.then_inc(exp_done, 1)

            def attention_step(i, j, first, last=False):
                n = STEPS * i + j
                if last and j == STEPS - 1:
                    sum_squares(0)
                if not first or j >= 1:
                    exponentials(n - 1)
                act.wait_ge(q_done, n + 1)
                nc.scalar.activation(qT[:], (R_PS if j == AHEAD else Q_PS)[:], copy).then_inc(q_sbuf, 1)
                if j == 0:
                    if not first:
                        act.wait_ge(k_done, n)
                    weights_high(ld_qk[1], 16 * i + 16, *qk_parts(1))
                if j == 2:
                    if not first:
                        act.wait_ge(wo_done, 2 * G * i)
                    weights_high(ld_o, 16 * i + 16, *o_parts())
                if j == 4 and not last:
                    act.wait_ge(k_done, n)
                    weights_high(ld_qk[0], 16 * i + 32, *qk_parts(0))
                if j == 5 and not last:
                    weights_high(ld_v, 16 * i + 32, *v_parts())
                if 1 <= j <= G:
                    for half in range(2):
                        act.wait_ge(v_done, 2 * G * i + 2 * (j - 1) + half + 1)
                        nc.scalar.activation(v_sb[:, tiles(j - 1, half), :], pair_of(VO_PS[half]), copy).then_inc(v_sbuf, 1)

            for j in range(STEPS):
                attention_step(0, j, True)
                if j < G:
                    affine(x2, lambda b: xs[:, TG * j + b, :], j, 0, ln2_ready, j + 1, x2_ready)
                elif j - 2 in LATE:
                    affine(xs, lambda b: xs[:, TG * (j - 2) + b, :], j - 2, 0, ln2_ready, j - 1, x2_ready)
                if j == 0:
                    for c in range(KD):
                        high(0, G - 1, c, PREP_PS[G - 1][c])
            with act.Fori(1, PAIRS - 1) as i:
                for j in range(STEPS):
                    attention_step(i, j, False)

            def exponentials_of_logits(g):
                act.wait_ge(centred, g + 1)
                nc.scalar.activation(logit[:, tiles(g), :], logit[:, tiles(g), :], ACT.Exp).then_inc(lexp_done, 1)

            def copy_logits(g):
                act.wait_ge(logit_done, g + 1)
                if g:
                    act.wait_ge(logit_T, g)
                nc.scalar.activation(logitT[:], R_PS[0:E, :], copy).then_inc(logit_sbuf, 1)

            def weight_rows(g):
                act.wait_ge(cw_T, g + 1)
                nc.scalar.activation(cwT[:, group_of(g)], R_PS[0:SELP, :], copy).then_inc(cwT_ready, 1)

            def expert_weights_high(body, j):
                act.wait_ge(ld_moe, body * 16 + 16)
                nc.scalar.activation(wm[0][j][:], raw_m[:, j, :], copy).then_inc(wm_hi_ready, 1)

            for j in range(STEPS):
                attention_step(PAIRS - 1, j, False, last=True)
                if j == 3:
                    act.wait_ge(ld_gate, 16)
                    nc.scalar.activation(gate_w[0][:], gate_raw[:], copy).then_inc(gate_split, 1)
                if 4 <= j < 4 + JB_EARLY:
                    expert_weights_high(0, j - 4)
            stream_root(0)
            act.wait_ge(scale_ready, 1)
            for b in range(TG):
                nc.scalar.activation(xn[:, b, :], xs[:, b, :], copy, scale=rstd[:, 0, b:b + 1]).then_inc(xn_ready, 1)
            exponentials(LAST - 1)
            high(1, 0, 0, R_PS)
            high(1, 0, 1, Q_PS)
            copy_logits(0)
            sum_squares(1)
            exponentials_of_logits(0)
            stream_root(1)
            act.wait_ge(wo_done, 2 * G * PAIRS)

            def expert_step(i, s, first, last=False):
                g, j, par = s // JB, s % JB, s % 2
                n = MSTEPS * i + s
                act.wait_ge(g_done, n + 1)
                if not first or s >= 2:
                    act.wait_ge(gated_ready, n - 1)
                nc.scalar.activation(silu[:, par, :], G_PS[par][:], ACT.Silu).then_inc(silu_ready, 1)
                if first and g + 1 < G and 1 <= j <= KD:
                    high(1, g + 1, j - 1, R_PS)
                if first and j == 0:
                    weight_rows(g)
                if first and g + 1 < G and j == 3:
                    copy_logits(g + 1)
                if shared(s, last):
                    act.wait_ge(gated_ready, n + 1)
                    act.wait_ge(d_done, n - 1)
                    nc.scalar.activation(hh[0][:, par, :], gated[:, par, :], copy).then_inc(hh_hi, 1)
                else:
                    act.wait_ge(hid_ready, weighed(i, s, last) + 1)
                    nc.scalar.activation(hh[0][:, par, :], hid[:, par, :], copy).then_inc(hh_hi, 1)
                if first and s < JB - JB_EARLY:
                    expert_weights_high(i, JB_EARLY + s)
                if s == 0 and not first:
                    act.wait_ge(d_done, n)
                    expert_weights_high(i, JB - 1)
                if s > MSTEPS - JB and not last:
                    act.wait_ge(d_done, n)
                    expert_weights_high(i + 1, j - 1)

            def root(g):
                square_root(3 * G + g + 1, g, TG)

            for s in range(MSTEPS):
                expert_step(0, s, True)
                g, j = s // JB, s % JB
                if j == 2 and g + 2 < G:
                    sum_squares(g + 2)
                if j == 3 and g + 1 < G:
                    exponentials_of_logits(g + 1)
                    if g + 2 < G:
                        stream_root(g + 2)
            with act.Fori(1, BODIES - 1) as i:
                for s in range(MSTEPS):
                    expert_step(i, s, False)
            for s in range(MSTEPS):
                expert_step(BODIES - 1, s, False, last=True)
                if s == 2 * JB + 1:
                    root(0)
                    root(1)
            root(G - 2)
            affine(xn, lambda b: xs[:, TG * (G - 2) + b, :], G - 2, 0, last_scaled, 1, applied)
            root(G - 1)

        @block.gpsimd
        def _(pool):
            def weights_low(value, raw, parts, ready):
                pool.wait_ge(w_hi_ready, value)
                nc.gpsimd.tensor_tensor(parts[1], raw, parts[0].bitcast(F32), ALU.subtract).then_inc(ready, 1)

            nc.gpsimd.memset(ones[:].bitcast(F32), 1.0).then_inc(bias_ready, 1)
            pool.wait_ge(ld_bias, 16)
            nc.gpsimd.tensor_copy(bias_part[0][:], bias_row[:]).then_inc(bias_ready, 1)
            pool.wait_ge(bias_ready, 2)
            nc.gpsimd.tensor_tensor(bias_part[1][:], bias_row[:], bias_part[0][:].bitcast(F32), ALU.subtract).then_inc(bias_ready, 1)
            weights_low(1, *qk_parts(0), qk_ready[0])
            weights_low(2, *v_parts(), v_ready)

            def normalise(n):
                pool.wait_ge(rinv_ready, n + 1)
                nc.gpsimd.tensor_tensor(prob[:], prob[:], rinv[:].rearrange("p (b o) -> p b o", o=1).to_broadcast([P, TG, S]),
                                        ALU.mult).then_inc(prob_ready, 1)

            def attention_step(i, j, first, last=False):
                n = STEPS * i + j
                if not first or j >= 1:
                    normalise(n - 1)
                if j == 0:
                    weights_low(4 * i + 3, *qk_parts(1), qk_ready[1])
                if j == 2:
                    weights_low(4 * i + 4, *o_parts(), o_ready)
                if j == 4 and not last:
                    weights_low(4 * i + 5, *qk_parts(0), qk_ready[0])
                if j == 5 and not last:
                    weights_low(4 * i + 6, *v_parts(), v_ready)

            for j in range(STEPS):
                attention_step(0, j, True)
            with pool.Fori(1, PAIRS - 1) as i:
                for j in range(STEPS):
                    attention_step(i, j, False)

            def expert_weights_low(body, j):
                pool.wait_ge(wm_hi_ready, body * JB + j + 1)
                nc.gpsimd.tensor_tensor(wm[1][j][:], raw_m[:, j, 0:WSPLIT], wm[0][j][:, 0:WSPLIT].bitcast(F32),
                                        ALU.subtract).then_inc(wm_ready, 1)

            def outer_residual(g):
                pool.wait_ge(xn_ready, NT + TG * (g + 1))
                for half in range(2):
                    nc.gpsimd.tensor_tensor(xs[:, tiles(g, half), :], xs[:, tiles(g, half), :], x2[:, tiles(g, half), :],
                                            ALU.add).then_inc(x_outer, 1)

            for j in range(STEPS):
                attention_step(PAIRS - 1, j, False, last=True)
                if 4 <= j < 4 + JB_EARLY:
                    expert_weights_low(0, j - 4)
            normalise(LAST - 1)
            for j in range(JB_EARLY, JB):
                expert_weights_low(0, j)
            for g in range(G):
                outer_residual(g)
            with pool.Fori(1, BODIES) as i:
                for j in range(JB):
                    expert_weights_low(i, j)

        @block.vector
        def _(dve):
            chain = [0]

            def link(ins):
                chain[0] += 1
                ins.then_inc(dve_chain, 1)
                dve.wait_ge(dve_chain, chain[0])

            def decay_weights():
                dve.wait_ge(ld_decay, 16 * 4)
                link(nc.vector.tensor_scalar(dv[:], dv[:], 0.9, 1.0, ALU.max, ALU.min))
                for c in range(KD):
                    nc.vector.tensor_tensor_scan(pow0[:, c, :], dv[:, 0:1].to_broadcast([P, D]), band[:, c, :], 0.0, ALU.mult, ALU.add)
                    link(nc.vector.tensor_tensor_scan(pow1[:, c, :], dv[:, 1:2].to_broadcast([P, D]), band[:, c, :], 0.0, ALU.mult, ALU.add))
                    link(nc.vector.tensor_tensor(pow1[:, c, :], pow1[:, c, :], w1_row[:], ALU.mult))
                    link(nc.vector.scalar_tensor_tensor(pow0[:, c, :], pow0[:, c, :], w0_col[:, c:c + 1], pow1[:, c, :],
                                                        ALU.mult, ALU.add))
                    nc.vector.tensor_tensor(wsum[:, c, :], pow0[:, c, :], band[:, c, :], ALU.add).then_inc(w_ready, 1)

            def running_sums(g):
                dve.wait_ge(ctx_sq, g + 1)
                for t in range(TG * g, TG * (g + 1)):
                    for c in range(KD):
                        ins = nc.vector.tensor_tensor_scan(run_sb[:, c, cols(t)], xdec[:, c:c + 1].to_broadcast([P, S]),
                                                           ctx_sb[:, c, cols(t)], 0.0, ALU.mult, ALU.add)
                ins.then_inc(run_ready, 1)

            def moments(g, src=lambda t: xs[:, t, :], ready=None):
                for t in range(TG * g, TG * (g + 1)):
                    if ready is not None and t % 2 == 0:
                        dve.wait_ge(ready, t // 2 + 1)
                    ins = nc.vector.bn_stats(stats[:, t, :], src(t))
                link(ins)
                for t in range(TG * g, TG * (g + 1)):
                    ins = nc.vector.bn_aggr(mv[:, t, :], stats[:, t, :])
                link(ins)

            def invert(g, w, times, refine=True, done=None):
                v, r = var[:, g, 0:w], rstd[:, g, 0:w]
                dve.wait_ge(std_ready, times)
                link(nc.vector.reciprocal(r, std[:, g, 0:w]))
                if refine:
                    link(nc.vector.tensor_tensor(v, v, r, ALU.mult))
                    link(nc.vector.tensor_tensor(v, v, r, ALU.mult))
                    link(nc.vector.tensor_scalar(v, v, -0.5 * ROOT_SCALE ** 1.5, 1.5 * ROOT_SCALE ** 0.5, ALU.mult, ALU.add))
                    ins = nc.vector.tensor_tensor(r, r, v, ALU.mult)
                    if done is None:
                        link(ins)
                    else:
                        ins.then_inc(done, 1)
                else:
                    link(nc.vector.tensor_scalar(r, r, ROOT_SCALE ** 0.5, None, ALU.mult))

            def shifts(g, at, done):
                nc.vector.scalar_tensor_tensor(shift[:, g, at:at + TG], mv[:, tiles(g), 0], -1.0,
                                               rstd[:, g, at:at + TG], ALU.mult, ALU.mult).then_inc(done, 1)

            def first_sum(g):
                moments(g, lambda t: PREP_PS[g][t % TG // 2][:, cols(t % 2, D)], ready=xw_done)
                nc.vector.tensor_scalar(var[:, g, 0:TG], mv[:, tiles(g), 1], LN_EPS, None, ALU.add).then_inc(var_ready, 1)

            def first_scale(g):
                invert(g, TG, var_order(1, g), refine=False)
                shifts(g, 0, ln1_ready)

            def second_sum(g):
                dve.wait_ge(x1_ready, TG * (g + 1))
                for half in range(2):
                    dve.wait_ge(run_T, 2 * g + half + 1)
                    nc.vector.scalar_tensor_tensor(xs[:, tiles(g, half), :], pair_of(PREP_PS[g][half]), 1.0,
                                                   xs[:, tiles(g, half), :], ALU.add, ALU.mult).then_inc(x_scanned, 1)
                moments(g, ready=x_scanned)
                nc.vector.tensor_scalar(var[:, g, TG:2 * TG], mv[:, tiles(g), 1], 1.0 + RMS_EPS, LN_EPS * RMS_EPS,
                                        ALU.mult, ALU.add)
                nc.vector.tensor_scalar(var[:, g, 0:TG], mv[:, tiles(g), 1], LN_EPS, None, ALU.add).then_inc(var_ready, 1)

            def second_scale(g):
                invert(g, 2 * TG, var_order(2, g))
                nc.vector.scalar_tensor_tensor(shift[:, g, 0:TG], mv[:, tiles(g), 0], -1.0, rstd[:, g, 0:TG], ALU.mult, ALU.mult)
                shifts(g, TG, ln2_ready)

            def low(norm, g, c, ps):
                dve.wait_ge(h_hi, norm * G * KD + KD * g + c + 1)
                nc.vector.scalar_tensor_tensor(hT[1][:, c, group_of(g)], ps[:], lnw[:, norm, c:c + 1],
                                               hT[0][:, c, group_of(g)].bitcast(F32), ALU.mult, ALU.subtract).then_inc(h_lo, 1)

            decay_weights()
            for g in range(G - 1):
                running_sums(g)
            for t in range(G + 3):
                if 3 <= t:
                    second_scale(t - 3)
                if 4 <= t:
                    for c in range(KD):
                        low(0, t - 4, c, PREP_PS[t - 4][c])
                if 2 <= t < G + 2:
                    second_sum(t - 2)
                if 1 <= t < G + 1:
                    first_scale(t - 1)
                if t < G:
                    first_sum(t)
                if t == 0:
                    running_sums(G - 1)

            def stream_variance(g):
                dve.wait_ge(squared, g + 1)
                nc.vector.tensor_scalar(var[:, g, 0:TG], mv[:, tiles(g), 0], 1.0 / D, RMS_EPS, ALU.mult, ALU.add).then_inc(var_ready, 1)

            def stream_scale(g):
                invert(g, TG, 2 * G + g + 1, done=scale_ready if g == 0 else None)
                if g == 0:
                    return
                for b in range(TG):
                    t = TG * g + b
                    nc.vector.tensor_scalar(xn[:, t, :], xs[:, t, :], rstd[:, g, b:b + 1], None, ALU.mult).then_inc(xn_ready, 1)

            def copy_probs(n):
                dve.wait_ge(pt_done, n + 1)
                nc.vector.tensor_copy(pT[:], PT_PS[:]).then_inc(pt_sbuf, 1)

            def row_bias(n):
                dve.wait_ge(s_done, n + 1)
                nc.vector.memset(pause[:], 0.0)
                for b in range(TG):
                    ins = nc.vector.tensor_tensor_reduce(prob[:, b, :], S_PS[:, cols(b)], mask[:], 1.0, LOWEST,
                                                         ALU.add, ALU.max, accum_out=rowmax[:, b:b + 1])
                ins.then_inc(masked, 1)
                dve.wait_ge(masked, n + 1)
                nc.vector.tensor_scalar(nbias[:], rowmax[:], -SCALE, None, ALU.mult).then_inc(nbias_ready, 1)

            def split_outputs(n, j):
                slot = j if j < G else G
                dve.wait_ge(o_done, n + 1)
                nc.vector.tensor_copy(oT[0][:, slot, :], O_PS[:]).then_inc(o_hi, 1)
                dve.wait_ge(o_hi, n + 1)
                nc.vector.tensor_tensor(oT[1][:, slot, :], O_PS[:], oT[0][:, slot, :].bitcast(F32),
                                        ALU.subtract).then_inc(o_lo, 1)

            def inverse_sum(n):
                dve.wait_ge(exp_done, n + 1)
                nc.vector.reciprocal(rinv[:], rowsum[:]).then_inc(rinv_ready, 1)

            def add_outputs(pair, g, first=False):
                for half in range(2):
                    if first:
                        dve.wait_ge(x2_ready, TG * (g + 1))
                    dve.wait_ge(wo_done, 2 * G * pair + 2 * g + half + 1)
                    nc.vector.tensor_tensor(xs[:, tiles(g, half), :], pair_of(VO_PS[half]), (x2 if first else xs)[:, tiles(g, half), :],
                                            ALU.add).then_inc(wo_added, 1)

            def attention_step(i, j, first, last=False):
                n = STEPS * i + j
                if not first or j >= 2:
                    copy_probs(n - 2)
                if not first or j >= 1:
                    row_bias(n - 1)
                if not first or j >= 2:
                    split_outputs(n - 2, (j - 2) % STEPS)
                if not first or j >= 1:
                    inverse_sum(n - 1)
                dve.wait_ge(k_done, n + 1)
                nc.vector.tensor_copy(kT[:], K_PS[:]).then_inc(k_sbuf, 1)
                if last and j == STEPS - 1:
                    stream_variance(0)
                    stream_scale(0)
                if j < 2 and not first:
                    add_outputs(i - 1, j + 2)
                if j >= 6:
                    add_outputs(i, j - 6, first)

            for j in range(STEPS):
                attention_step(0, j, True)
                if j == 0:
                    for c in range(KD):
                        low(0, G - 1, c, PREP_PS[G - 1][c])
            dve.wait_ge(x2_ready, TG * (G + len(LATE)))
            with dve.Fori(1, PAIRS - 1) as i:
                for j in range(STEPS):
                    attention_step(i, j, False)

            def per_tile(ap):
                return ap.rearrange("p (t o) -> p t o", o=1).to_broadcast([P, TG, E])

            def centre(g):
                dve.wait_ge(logit_T, g + 1)
                found = R_PS[:, 0:TG * E].rearrange("p (t e) -> p t e", e=E)
                link(nc.vector.tensor_reduce(lmax[:, tiles(g)], found, mybir.AxisListType.X, ALU.max))
                nc.vector.tensor_tensor(logit[:, tiles(g), :], found, per_tile(lmax[:, tiles(g)]), ALU.subtract).then_inc(centred, 1)

            def route(g):
                ts = tiles(g)
                dve.wait_ge(lexp_done, g + 1)
                link(nc.vector.tensor_reduce(lsum[:, ts], logit[:, ts, :], mybir.AxisListType.X, ALU.add))
                link(nc.vector.reciprocal(lsum[:, ts], lsum[:, ts]))
                link(nc.vector.tensor_tensor(logit[:, ts, :], logit[:, ts, :], per_tile(lsum[:, ts]), ALU.mult))
                for t in range(TG * g, TG * (g + 1)):
                    ins = nc.vector.max(best[:, t, :], logit[:, t, :])
                link(ins)
                link(nc.vector.memset(best[:, ts, TOPK:8], -1.0))
                for t in range(TG * g, TG * (g + 1)):
                    ins = nc.vector.match_replace(rest[:, t, :], best[:, t, :], logit[:, t, :], 0.0)
                link(ins)
                link(nc.vector.tensor_tensor(cw[:, ts, :], logit[:, ts, :], rest[:, ts, :], ALU.subtract))
                link(nc.vector.tensor_reduce(csum[:, ts], cw[:, ts, :], mybir.AxisListType.X, ALU.add))
                link(nc.vector.reciprocal(csum[:, ts], csum[:, ts]))
                link(nc.vector.tensor_tensor(cw[:, ts, :], cw[:, ts, :], per_tile(csum[:, ts]), ALU.mult))
                link(nc.vector.tensor_copy(cw_hi[:, ts, :], cw[:, ts, :]))
                nc.vector.tensor_copy(cw_rows[:, ts, 0:E], cw_hi[:, ts, :].bitcast(F32))
                nc.vector.tensor_tensor(cw_rows[:, ts, E:SELP], cw[:, ts, :], cw_hi[:, ts, :].bitcast(F32),
                                        ALU.subtract).then_inc(cw_ready, 1)

            for j in range(STEPS):
                attention_step(PAIRS - 1, j, False, last=True)
                if j == 4:
                    dve.wait_ge(gate_split, 1)
                    nc.vector.tensor_tensor(gate_w[1][:], gate_raw[:], gate_w[0][:].bitcast(F32), ALU.subtract).then_inc(gate_split, 1)
            copy_probs(LAST - 2)
            row_bias(LAST - 1)
            split_outputs(LAST - 2, STEPS - 2)
            inverse_sum(LAST - 1)
            low(1, 0, 0, R_PS)
            low(1, 0, 1, Q_PS)
            add_outputs(PAIRS - 1, 2)
            copy_probs(LAST - 1)
            centre(0)
            split_outputs(LAST - 1, STEPS - 1)
            stream_variance(1)
            route(0)
            add_outputs(PAIRS - 1, 3)
            stream_scale(1)

            def add_group(count, g, ready=None):
                if ready is not None:
                    dve.wait_ge(x_outer, ready)
                dve.wait_ge(d_done, count)
                for half in range(2):
                    ins = nc.vector.tensor_tensor(xs[:, tiles(g, half), :], pair_of(ACC_PS[half]), xs[:, tiles(g, half), :], ALU.add)
                ins.then_inc(acc_added, 1)

            def expert_step(i, s, first, last=False):
                g, j, par = s // JB, s % JB, s % 2
                n = MSTEPS * i + s
                dve.wait_ge(silu_ready, n + 1)
                dve.wait_ge(u_done, n + 1)
                nc.vector.tensor_tensor(gated[:, par, :], U_PS[par][:], silu[:, par, :], ALU.mult).then_inc(gated_ready, 1)
                if first and g + 1 < G:
                    if 1 <= j <= KD:
                        low(1, g + 1, j - 1, R_PS)
                    if j == 3:
                        if g + 2 < G:
                            stream_variance(g + 2)
                if not shared(s, last):
                    dve.wait_ge(gated_ready, n + 1)
                    dve.wait_ge(c_done, weighed(i, s, last) + 1)
                    nc.vector.tensor_tensor(hid[:, par, :], CW_PS[:], gated[:, par, :], ALU.mult).then_inc(hid_ready, 1)
                if j == 0 and (not first or g >= 1):
                    add_group(n, (g - 1) % G, 2 * g if first else None)
                dve.wait_ge(hh_hi, n + 1)
                nc.vector.tensor_tensor(hh[1][:, par, :], (gated if shared(s, last) else hid)[:, par, :], hh[0][:, par, :].bitcast(F32),
                                        ALU.subtract).then_inc(hh_lo, 1)

            def last_moments(g):
                dve.wait_ge(acc_added, G * (BODIES - 1) + g + 1)
                moments(g)
                last_variance(g)

            def last_variance(g):
                nc.vector.tensor_scalar(var[:, g, 0:TG], mv[:, tiles(g), 1], LN_EPS, None, ALU.add).then_inc(var_ready, 1)

            def last_sum():
                for half in range(2):
                    if half:
                        dve.wait_ge(d_done, MLAST)
                    else:
                        dve.wait_ge(d_half, 1)
                    link(nc.vector.tensor_tensor(xs[:, tiles(G - 1, half), :], pair_of(ACC_PS[half]), xs[:, tiles(G - 1, half), :], ALU.add))
                    for t in range(2):
                        b = TG * (G - 1) + 2 * half + t
                        ins = nc.vector.bn_stats(stats[:, b, :], xs[:, b, :])
                link(ins)
                for t in range(NT - TG, NT):
                    ins = nc.vector.bn_aggr(mv[:, t, :], stats[:, t, :])
                link(ins)
                last_variance(G - 1)

            def last_layernorm(g):
                invert(g, TG, 3 * G + g + 1)
                for b in range(TG):
                    t = TG * g + b
                    nc.vector.tensor_scalar(xn[:, t, :], xs[:, t, :], mv[:, t, 0:1], rstd[:, g, b:b + 1],
                                            ALU.subtract, ALU.mult).then_inc(final_ready, 1)

            for s in range(MSTEPS):
                expert_step(0, s, True)
                g, j = s // JB, s % JB
                if j == 3 and g + 1 < G:
                    centre(g + 1)
                    route(g + 1)
                if j == 4 and g + 2 < G:
                    stream_scale(g + 2)
            dve.wait_ge(x_outer, 2 * G)
            with dve.Fori(1, BODIES - 1) as i:
                for s in range(MSTEPS):
                    expert_step(i, s, False)
            for s in range(MSTEPS):
                expert_step(BODIES - 1, s, False, last=True)
                if s >= JB and s % JB == 0:
                    last_moments(s // JB - 1)
                if s in (2 * JB + 2, 2 * JB + 3):
                    last_layernorm(s - 2 * JB - 2)
            invert(G - 2, TG, 3 * G + G - 1)
            shifts(G - 2, 0, last_scaled)
            last_sum()
            last_layernorm(G - 1)


def _program(nc, args, out):
    decoder_layer(nc, *args, out)


def kernel(**inputs):
    import numpy as np
    import concourse.bacc as bacc
    from concourse.bass_utils import run_bass_kernel_spmd as run

    a = {k: np.asarray(v) for k, v in inputs.items()}
    f32 = np.float32
    tokens = B * S
    xT = a["x"].reshape(tokens, D).T
    ctxT = a["ctx_2048"].reshape(tokens, D).T
    bands = np.eye(D, dtype=f32).reshape(KD, P, D).transpose(1, 0, 2)
    ident = np.eye(P, dtype=f32)
    mask = np.where(np.arange(S)[None, :] <= np.arange(S)[:, None], 0.0, -1e9 * float(HD) ** 0.5).astype(f32)
    def chunks(w, lo, n):
        return w[:, lo:lo + n].reshape(KD, P, n).transpose(1, 0, 2).reshape(P, KD * n)
    att = np.empty((PAIRS, P, 2 * 2 * KD * HD + KD * 2 * HD + 2 * D), f32)
    for p in range(PAIRS):
        parts = []
        for h in (2 * p, 2 * p + 1):
            parts += [chunks(a["L0_ffn_wq"], HD * h, HD), chunks(a["L0_ffn_wk"], HD * h, HD)]
        parts.append(chunks(a["L0_ffn_wv"], 2 * HD * p, 2 * HD))
        parts.append(a["L0_ffn_wo"][2 * HD * p:2 * HD * (p + 1)].reshape(2, HD, D).transpose(1, 0, 2).reshape(P, 2 * D))
        att[p] = np.concatenate(parts, axis=1)
    pad = CT * P - E * I - SI
    def flat(routed, shared):
        return np.concatenate([routed, shared, np.zeros((pad, D), f32)], axis=0)
    wg = flat(a["L0_ffn_eg_w"].reshape(E * I, D), a["L0_ffn_sg_w"])
    wu = flat(a["L0_ffn_eu_w"].reshape(E * I, D), a["L0_ffn_su_w"])
    wd = flat(a["L0_ffn_ed_w"].transpose(0, 2, 1).reshape(E * I, D), a["L0_ffn_sd_w"].T)
    channel = np.arange(E * I)
    sel = np.zeros((P, CT * P), f32)
    sel[channel // I, channel] = 1.0
    sel[E + channel // I, channel] = 1.0
    moe = np.concatenate([chunks(wg.T, 0, CT * P).reshape(P, KD, CT, P).transpose(0, 2, 1, 3).reshape(P, CT, KD * P),
                          chunks(wu.T, 0, CT * P).reshape(P, KD, CT, P).transpose(0, 2, 1, 3).reshape(P, CT, KD * P),
                          wd.reshape(CT, P, D).transpose(1, 0, 2),
                          sel.reshape(P, CT, P)], axis=2)
    moe = moe.reshape(P, BODIES, JB, WT).transpose(1, 0, 2, 3)
    columns = np.stack([a["L0_attn_weight"][0], np.repeat(a["L0_xattn_decay"].reshape(-1), D // a["L0_xattn_decay"].size),
                        a["L0_ffn_ln1_w"], a["L0_ffn_ln2_w"]]).reshape(4, KD, P).transpose(2, 0, 1)
    arrays = {
        "xT": xT, "ctxT": ctxT, "bands": bands, "ident": ident, "mask": mask,
        "aw": a["L0_attn_weight"], "bias": a["L0_attn_bias"], "decay": a["L0_attn_decay_value"].reshape(2),
        "columns": columns, "w_att": att,
        "gateT": a["L0_ffn_gate_w"].T.reshape(KD, P, E).transpose(1, 0, 2), "w_moe": moe,
    }
    arrays = {k: np.ascontiguousarray(v) for k, v in arrays.items()}
    nc = bacc.Bacc("TRN2", target_bir_lowering=False, num_devices=1)
    args = [nc.dram_tensor(f"in_{k}", v.shape, mybir.dt.from_np(v.dtype), kind="ExternalInput").ap()
            for k, v in arrays.items()]
    out = nc.dram_tensor("out_x", (B, S, D), F32, kind="ExternalOutput").ap()
    _program(nc, args, out)
    r = run(nc, [{f"in_{k}": v for k, v in arrays.items()}], core_ids=[0])
    return r.results[0]["out_x"]
```
